# Optimizing a Trainium2 kernel written in Bass

```python
import numpy as np
import jax
import jax.numpy as jnp

def _softmax(x, axis=-1):
    return jax.nn.softmax(x, axis=axis)

def _gelu(x):
    return jax.nn.gelu(x, approximate=True)

def _silu(x):
    return jax.nn.silu(x)

def _sigmoid(x):
    return jax.nn.sigmoid(x)

def _layernorm(x, axis=-1, eps=1e-05):
    m = jnp.mean(x, axis=axis, keepdims=True)
    v = jnp.var(x, axis=axis, keepdims=True)
    return (x - m) / jnp.sqrt(v + eps)

def _scatter_add(tgt, idx, src, axis=0):
    return tgt.at[idx].add(src)

def _segment_sum(src, seg, n):
    return jax.ops.segment_sum(src, seg, n)
kernel_name = 'mk_perceiver_d1_seqx_r4_c0166e'

def setup_inputs(seed: int=0):
    np.random.seed(seed)
    _w = jnp.asarray

    def _rec_inputs():
        import jax
        import jax.numpy as jnp
        _rk = jax.random.key(seed)
        x = 7.22e-05 + 1 * jax.random.normal(jax.random.fold_in(_rk, 1), (8, 64, 256), jnp.float32)
        _lenS = 64 - jax.random.randint(jax.random.fold_in(_rk, 7), (8,), 0, max(1, 64 // 4) + 1, jnp.int32)
        _lenS2 = 1601 - jax.random.randint(jax.random.fold_in(_rk, 8), (8,), 0, max(1, 1601 // 4) + 1, jnp.int32)
        _ctx_768P = jax.random.normal(jax.random.fold_in(_rk, 11), (8, 16, 192), jnp.float32)
        _ctx_768c = jax.random.dirichlet(jax.random.fold_in(_rk, 511), 0.3 * jnp.ones((16,), jnp.float32), (8, 1601))
        _ctx_768t = jnp.einsum('bsk,bkd->bsd', _ctx_768c, _ctx_768P)
        _ctx_768t = _ctx_768t * jax.lax.rsqrt(jnp.mean(jnp.square(_ctx_768t)) + 1e-12) * 0.953939
        ctx_768 = 2.09791e-05 + 1.00001 * (_ctx_768t + 0.3 * jax.random.normal(jax.random.fold_in(_rk, 611), (8, 1601, 192), jnp.float32))
        return (x, ctx_768)
    x, ctx_768 = _rec_inputs()

    def _L0_xattn_setup():
        import jax, jax.numpy as jnp
        import numpy as np
        HEADS = 16
        DIM_HEAD = 64
        key = jax.random.key(seed)
        ks = jax.random.split(key, 7)
        B, Nq, Dq = (4, 512, 256)
        Nk, Dc = (256, 192)
        inner = HEADS * DIM_HEAD
        sq = 1.0 / np.sqrt(Dq)
        sc = 1.0 / np.sqrt(Dc)
        si = 1.0 / np.sqrt(inner)
        return {'x': jax.random.normal(ks[0], (B, Nq, Dq), dtype=jnp.float32), 'context': jax.random.normal(ks[1], (B, Nk, Dc), dtype=jnp.float32), 'Wq': jax.random.normal(ks[2], (Dq, inner), dtype=jnp.float32) * sq, 'Wk': jax.random.normal(ks[3], (Dc, inner), dtype=jnp.float32) * sc, 'Wv': jax.random.normal(ks[4], (Dc, inner), dtype=jnp.float32) * sc, 'Wo': jax.random.normal(ks[5], (inner, Dq), dtype=jnp.float32) * si, 'bo': jax.random.normal(ks[6], (Dq,), dtype=jnp.float32) * 0.01}
    _L0_xattn_all = _L0_xattn_setup()
    _L0_xattn_in = {k: v for k, v in _L0_xattn_all.items() if k in ('Wq', 'Wk', 'Wv', 'Wo', 'bo')}
    del _L0_xattn_all

    def _L0_attn_setup():
        import jax, jax.numpy as jnp
        import numpy as np
        DIM = 256
        CHUNK = 64
        STATE = 64
        DT_RANK = (DIM + 15) // 16
        EPS = 1e-06

        def _rmsnorm(x, w):
            var = jnp.mean(x * x, axis=-1, keepdims=True)
            return x * jax.lax.rsqrt(var + EPS) * w
        key = jax.random.key(seed)
        ks = jax.random.split(key, 6)
        B, L = (2, 1024)
        x = jax.random.normal(ks[0], (B, L, DIM), dtype=jnp.float32)
        norm_w = jnp.ones((DIM,), dtype=jnp.float32)
        x_proj_w = jax.random.normal(ks[1], (DT_RANK + 2 * STATE, DIM), dtype=jnp.float32) * 0.02
        dt_proj_w = jax.random.normal(ks[2], (DIM, DT_RANK), dtype=jnp.float32) * 0.02
        dt_proj_b = jnp.zeros((DIM,), dtype=jnp.float32)
        A_log = jnp.zeros((DIM, STATE), dtype=jnp.float32)
        D = jnp.ones((DIM,), dtype=jnp.float32)
        out_proj_w = jax.random.normal(ks[3], (DIM, DIM), dtype=jnp.float32) * 0.02
        return {'x': x, 'norm_w': norm_w, 'x_proj_w': x_proj_w, 'dt_proj_w': dt_proj_w, 'dt_proj_b': dt_proj_b, 'A_log': A_log, 'D': D, 'out_proj_w': out_proj_w}
    _L0_attn_all = _L0_attn_setup()
    _L0_attn_in = {k: v for k, v in _L0_attn_all.items() if k in ('norm_w', 'x_proj_w', 'dt_proj_w', 'dt_proj_b', 'A_log', 'D', 'out_proj_w')}
    del _L0_attn_all

    def _L0_ffn_setup():
        import jax, jax.numpy as jnp
        import numpy as np
        BLOCK_SIZE = 32
        FP6_E2M3_MAX = 7.5

        def _build_fp6_e2m3_grid():
            vals = set()
            for bits in range(64):
                s = bits >> 5 & 1
                e = bits >> 3 & 3
                m = bits & 7
                v = m / 8.0 if e == 0 else (1.0 + m / 8.0) * 2.0 ** (e - 1)
                vals.add(-v if s else v)
            return np.array(sorted(vals), dtype=np.float32)
        _GRID = jnp.asarray(_build_fp6_e2m3_grid())

        def _nearest_on_grid(x, grid):
            idx = jnp.clip(jnp.searchsorted(grid, x), 0, grid.shape[0] - 1)
            idx_lo = jnp.maximum(idx - 1, 0)
            v_hi = grid[idx]
            v_lo = grid[idx_lo]
            return jnp.where(jnp.abs(x - v_lo) <= jnp.abs(x - v_hi), v_lo, v_hi)

        def _mx_quantize(t, eps=1e-30):
            rows, K = t.shape
            blocks = t.reshape(rows, K // BLOCK_SIZE, BLOCK_SIZE)
            scales = jnp.maximum(jnp.max(jnp.abs(blocks), axis=-1) / FP6_E2M3_MAX, eps)
            q = _nearest_on_grid(blocks / scales[..., None], _GRID)
            return (q, scales)
        key = jax.random.key(seed)
        k1, k2, k3 = jax.random.split(key, 3)
        x = jax.random.normal(k1, (8, 2048, 256), dtype=jnp.float32)
        weight = jax.random.normal(k2, (256, 256), dtype=jnp.float32) * 0.02
        bias = jax.random.normal(k3, (256,), dtype=jnp.float32) * 0.02
        return {'x': x, 'weight': weight, 'bias': bias}
    _L0_ffn_all = _L0_ffn_setup()
    _L0_ffn_in = {k: v for k, v in _L0_ffn_all.items() if k in ('weight', 'bias')}
    del _L0_ffn_all
    return {'x': x, 'ctx_768': ctx_768, 'L0_xattn_Wq': _L0_xattn_in['Wq'], 'L0_xattn_Wk': _L0_xattn_in['Wk'], 'L0_xattn_Wv': _L0_xattn_in['Wv'], 'L0_xattn_Wo': _L0_xattn_in['Wo'], 'L0_xattn_bo': _L0_xattn_in['bo'], 'L0_attn_norm_w': _L0_attn_in['norm_w'], 'L0_attn_x_proj_w': _L0_attn_in['x_proj_w'], 'L0_attn_dt_proj_w': _L0_attn_in['dt_proj_w'], 'L0_attn_dt_proj_b': _L0_attn_in['dt_proj_b'], 'L0_attn_A_log': _L0_attn_in['A_log'], 'L0_attn_D': _L0_attn_in['D'], 'L0_attn_out_proj_w': _L0_attn_in['out_proj_w'], 'L0_ffn_weight': _L0_ffn_in['weight'], 'L0_ffn_bias': _L0_ffn_in['bias']}

def reference(x, ctx_768, L0_xattn_Wq, L0_xattn_Wk, L0_xattn_Wv, L0_xattn_Wo, L0_xattn_bo, L0_attn_norm_w, L0_attn_x_proj_w, L0_attn_dt_proj_w, L0_attn_dt_proj_b, L0_attn_A_log, L0_attn_D, L0_attn_out_proj_w, L0_ffn_weight, L0_ffn_bias):
    import jax
    import jax.numpy as jnp

    def _L0_xattn_ref(x, context, Wq, Wk, Wv, Wo, bo):
        import jax, jax.numpy as jnp
        import numpy as np
        HEADS = 16
        DIM_HEAD = 64
        B, Nq, _ = x.shape
        Nk = context.shape[1]
        h, dh = (HEADS, DIM_HEAD)
        q = (x @ Wq).reshape(B, Nq, h, dh)
        k = (context @ Wk).reshape(B, Nk, h, dh)
        v = (context @ Wv).reshape(B, Nk, h, dh)
        scale = 1.0 / jnp.sqrt(jnp.asarray(dh, dtype=x.dtype))
        scores = jnp.einsum('bqhd,bkhd->bhqk', q, k) * scale
        attn = jax.nn.softmax(scores, axis=-1)
        out = jnp.einsum('bhqk,bkhd->bqhd', attn, v).reshape(B, Nq, h * dh)
        return out @ Wo + bo

    def _L0_attn_ref(x, norm_w, x_proj_w, dt_proj_w, dt_proj_b, A_log, D, out_proj_w):
        import jax, jax.numpy as jnp
        import numpy as np
        DIM = 256
        CHUNK = 64
        STATE = 64
        DT_RANK = (DIM + 15) // 16
        EPS = 1e-06

        def _rmsnorm(x, w):
            var = jnp.mean(x * x, axis=-1, keepdims=True)
            return x * jax.lax.rsqrt(var + EPS) * w
        B, L, Dm = x.shape
        assert L % CHUNK == 0
        nc = L // CHUNK
        M = B * nc
        xn = _rmsnorm(x, norm_w)
        proj = jnp.einsum('bld,pd->blp', xn, x_proj_w)
        delta_lo, Bs, Cs = jnp.split(proj, [DT_RANK, DT_RANK + STATE], axis=-1)
        delta = jax.nn.softplus(jnp.einsum('blr,dr->bld', delta_lo, dt_proj_w) + dt_proj_b)
        A = -jnp.exp(A_log)

        def to_tm(t, feat):
            return t.reshape(B, nc, CHUNK, feat).reshape(M, CHUNK, feat).transpose(1, 0, 2)
        dt_seq = to_tm(delta, Dm)
        b_seq = to_tm(Bs, STATE)
        c_seq = to_tm(Cs, STATE)
        x_seq = to_tm(xn, Dm)

        def step(h, inp):
            dt, bt, ct, xt = inp
            dA = jnp.exp(dt[..., None] * A)
            h = dA * h + dt[..., None] * bt[:, None, :] * xt[..., None]
            y = jnp.einsum('mdn,mn->md', h, ct)
            return (h, y)
        h0 = jnp.zeros((M, Dm, STATE), dtype=x.dtype)
        _, ys = jax.lax.scan(step, h0, (dt_seq, b_seq, c_seq, x_seq))
        y = ys.transpose(1, 0, 2).reshape(B, nc, CHUNK, Dm).reshape(B, L, Dm)
        return jnp.einsum('bld,od->blo', y + x * D, out_proj_w)

    def _L0_ffn_ref(x, weight, bias):
        import jax, jax.numpy as jnp
        import numpy as np
        BLOCK_SIZE = 32
        FP6_E2M3_MAX = 7.5

        def _build_fp6_e2m3_grid():
            vals = set()
            for bits in range(64):
                s = bits >> 5 & 1
                e = bits >> 3 & 3
                m = bits & 7
                v = m / 8.0 if e == 0 else (1.0 + m / 8.0) * 2.0 ** (e - 1)
                vals.add(-v if s else v)
            return np.array(sorted(vals), dtype=np.float32)
        _GRID = jnp.asarray(_build_fp6_e2m3_grid())

        def _nearest_on_grid(x, grid):
            idx = jnp.clip(jnp.searchsorted(grid, x), 0, grid.shape[0] - 1)
            idx_lo = jnp.maximum(idx - 1, 0)
            v_hi = grid[idx]
            v_lo = grid[idx_lo]
            return jnp.where(jnp.abs(x - v_lo) <= jnp.abs(x - v_hi), v_lo, v_hi)

        def _mx_quantize(t, eps=1e-30):
            rows, K = t.shape
            blocks = t.reshape(rows, K // BLOCK_SIZE, BLOCK_SIZE)
            scales = jnp.maximum(jnp.max(jnp.abs(blocks), axis=-1) / FP6_E2M3_MAX, eps)
            q = _nearest_on_grid(blocks / scales[..., None], _GRID)
            return (q, scales)
        batch_shape = x.shape[:-1]
        in_features = x.shape[-1]
        x2 = x.astype(jnp.float32).reshape(-1, in_features)
        w2 = weight.astype(jnp.float32)
        xq, xs = _mx_quantize(x2)
        wq, ws = _mx_quantize(w2)
        xd = (xq * xs[..., None]).reshape(x2.shape)
        wd = (wq * ws[..., None]).reshape(w2.shape)
        out = xd @ wd.T + bias
        return out.reshape(*batch_shape, -1)
    x = x + _L0_xattn_ref(_layernorm(x, axis=-1), ctx_768, L0_xattn_Wq, L0_xattn_Wk, L0_xattn_Wv, L0_xattn_Wo, L0_xattn_bo)
    x = x + _L0_attn_ref(_layernorm(x, axis=-1), L0_attn_norm_w, L0_attn_x_proj_w, L0_attn_dt_proj_w, L0_attn_dt_proj_b, L0_attn_A_log, L0_attn_D, L0_attn_out_proj_w)
    x = x + _L0_ffn_ref(_layernorm(x, axis=-1), L0_ffn_weight, L0_ffn_bias)
    return x

_drawn_inputs = setup_inputs


def setup_inputs(seed=0):
    import zlib

    import numpy as np

    out = dict(_drawn_inputs(seed))
    spreads = {'L0_attn_norm_w': (1.0, 0.2),
     'L0_attn_dt_proj_b': (0.0, 0.47),
     'L0_attn_A_log': (0.0, 0.556),
     'L0_attn_D': (1.0, 0.2)}
    factors = {'L0_xattn_bo': 5.395, 'L0_attn_dt_proj_w': 8.0, 'L0_ffn_bias': 3.536}
    for name, (base, spread) in spreads.items():
        noise = np.random.default_rng([zlib.crc32(name.encode()), seed]).standard_normal(out[name].shape)
        drawn = base * np.exp(spread * noise) if base else spread * noise
        out[name] = jnp.asarray(drawn.astype(out[name].dtype))
    for name, factor in factors.items():
        out[name] = (out[name] * factor).astype(out[name].dtype)
    return out
```

```python
from contextlib import ExitStack

import concourse.bass as bass
from concourse import mybir

F32 = mybir.dt.float32
F32R = mybir.dt.float32r
ALU = mybir.AluOpType
ACT = mybir.ActivationFunctionType
AX = mybir.AxisListType

P = 128
LN_EPS = 1e-5
RMS_EPS = 1e-6
FP6_MAX = 7.5
FP6_BLOCK = 32
SCALE_FLOOR = 1e-30
ROUND = 1.5 * 2.0 ** 23

FIRST, LOOP_FROM, LOOP_TO, LAST = -1, 3, 7, 10


def perceiver_layer(nc, x, ctx, Wq, Wk, Wv, Wo, bo, norm_w, x_proj_w, dt_proj_w, dt_proj_b,
                    A_log, D, out_proj_w, ffn_w, ffn_b, out):
    NB, NQ, DM = x.shape
    NK, DC = ctx.shape[1], ctx.shape[2]
    INNER = Wq.shape[1]
    DH = 64
    TILES = INNER // P
    NT = NB * TILES
    DT = DC - P
    KT = -(-NK // P)
    KLAST = NK - (KT - 1) * P
    NKP = NK + NK % 2
    GROUPS = [(g, min(4, KT - g)) for g in range(0, KT, 4)]
    CHUNKS = [(c, min(512, NK - c)) for c in range(0, NK, 512)]
    NG = len(GROUPS)
    RH, RW = DC + 2, 2 * DC + 2
    STATE = A_log.shape[1]
    RANK = dt_proj_w.shape[1]
    NS = 16
    SLICES = 2 * STATE // NS
    SG = STATE // NS
    RT = NB * NQ // P
    assert NG == len(CHUNKS) == SG == 4 and TILES == SLICES == NB == 8 and NQ == DH and DM == 2 * P

    es = ExitStack()
    with es:
        def sb(name, shape, dt=F32):
            return es.enter_context(nc.sbuf_tensor(name, shape, dt))

        def sem(name):
            return es.enter_context(nc.semaphore(name))

        ident = sb("ident", [P, P])
        wkT = sb("wkT", [P, TILES, DC])
        wv_a = sb("wv_a", [P, INNER])
        wv_b = sb("wv_b", [DT, INNER])
        wo = sb("wo", [P, TILES, DM])
        xpT = sb("xpT", [P, 2, RANK + 2 * STATE])
        dtwT = sb("dtwT", [RANK, DM])
        opT = sb("opT", [P, 2, DM])
        wdT = sb("wdT", [P, 2, DM])
        negA = sb("negA", [P, 2, STATE])
        cols = sb("cols", [P, 3, 2])
        norm_c, dtb_c, D_c = cols[:, 0, :], cols[:, 1, :], cols[:, 2, :]
        one_c = sb("one_c", [P, 1])
        bias_r = sb("bias_r", [P, DM])
        bo_r = sb("bo_r", [P, DM])
        x_rows = sb("x_rows", [P, RT, DM])

        raw = [sb(f"raw{i}", [P, 4, P + 2 * DT]) for i in range(2)]
        rows = [sb(f"rows{i}", [P, KT, RW], F32R) for i in range(2)]
        ctH = [sb(f"ctH{i}", [P, NKP], F32R) for i in range(2)]
        ctL = [sb(f"ctL{i}", [P, NKP], F32R) for i in range(2)]
        ctT = [sb(f"ctT{i}", [P, NKP], F32R) for i in range(2)]
        qd = [sb(f"qd{i}", [P, TILES, P]) for i in range(2)]
        qpH = [sb(f"qpH{i}", [P, 2, P], F32R) for i in range(2)]
        qpL = [sb(f"qpL{i}", [P, 2, P], F32R) for i in range(2)]
        cmax = sb("cmax", [P, NG])
        nmax = sb("nmax", [P, 2])
        prob = sb("prob", [P, NK])
        ptH = [sb(f"ptH{i}", [P, 4, P], F32R) for i in range(2)]
        ptL = [sb(f"ptL{i}", [P, 4, P], F32R) for i in range(2)]
        rinv = sb("rinv", [P, 1])
        olow = sb("olow", [P, DC])
        osb = [sb(f"osb{i}", [P, DC]) for i in range(2)]
        oT = sb("oT", [P, 2, P])
        ao = [sb(f"ao{i}", [P, TILES, NQ]) for i in range(2)]

        st = sb("st", [P, RT, 6])
        mv = sb("mv", [P, RT, 2])
        ve = sb("ve", [P, RT])
        rs0 = sb("rs0", [P, RT])
        rs1 = sb("rs1", [P, RT])
        xln = sb("xln", [P, 2, DM])
        xnT = sb("xnT", [P, 2, NQ])
        bc = sb("bc", [P, NQ])
        dlo = sb("dlo", [RANK, NQ])
        zdt = sb("zdt", [P, 2, NQ])
        sp1 = sb("sp1", [P, 2, NQ])
        dt_ = [sb(f"dt{i}", [P, 2, NQ]) for i in range(2)]
        dtx = [sb(f"dtx{i}", [P, 2, NQ]) for i in range(2)]
        ypart = [sb(f"ypart{i}", [P, 2, SG + 1, NQ]) for i in range(2)]
        yT = sb("yT", [P, 2, NQ])
        bcr = [sb(f"bcr{i}", [P, 2, NS * NQ]) for i in range(2)]
        dA = [sb(f"dA{i}", [P, NS, NQ]) for i in range(2)]
        hs = [sb(f"hs{i}", [P, NS, NQ]) for i in range(2)]

        bank = [es.enter_context(nc.psum_tensor(f"bank{i}", [P, 512], F32)) for i in range(8)]
        pt_bank = [bank[4], bank[5]]
        o_bank = bank[6]
        misc = bank[7]
        bc_scratch = nc.dram_tensor("bc_scratch", [NB, P, NQ], F32, kind="Internal").ap()
        q_scratch = nc.dram_tensor("q_scratch", [NB, P, TILES, NQ], F32, kind="Internal").ap()

        def flat(t):
            return t[:] if len(t.shape) == 2 else t[:].rearrange("p a b -> p (a b)")

        wq_v = [flat(dA[0]), flat(dA[1])]
        wk_a, wk_b = flat(hs[0]), flat(hs[1])[0:DT, :]
        x0 = bcr[0][:, 0, :].rearrange("p (r d) -> p r d", r=RT)
        xT0 = bcr[0][:, 1, :].rearrange("p (h n) -> p h n", h=2)
        op_rows = bcr[1][:, 0, 0:2 * DM].rearrange("p (h d) -> p h d", h=2)
        fw_rows = bcr[1][:, 0, 2 * DM:4 * DM].rearrange("p (h d) -> p h d", h=2)
        q_stage = [bcr[1][:, 1, 512 * i:512 * i + 512] for i in range(2)]
        yp0, yp1 = [y[:].rearrange("p a b c -> p (a b c)") for y in ypart]
        xp_bc, xp_dt = yp0[:, 0:DM], yp0[0:RANK, DM:2 * DM]
        dtw_rows = yp1[:, 0:2 * RANK].rearrange("p (h r) -> p h r", h=2)

        s_wq, s_wk, s_w, s_x = sem("wq_loaded"), sem("wk_loaded"), sem("weights_loaded"), sem("x_loaded")
        s_raw = [sem("raw_loaded0"), sem("raw_loaded1")]
        s_id0, s_ident = sem("ident_cleared"), sem("ident_ready")
        s_ope = [sem("open_psum_act"), sem("open_psum_dve")]
        s_oev = [sem("open_copied_act"), sem("open_copied_dve")]
        s_odve, s_oact = sem("open_dve"), sem("open_act")
        s_qst = [sem("q_stored0"), sem("q_stored1")]
        s_opened = sem("opened")
        s_qd = [sem("queries_placed0"), sem("queries_placed1")]
        s_qp, s_qpH = sem("qprime_summed"), sem("qprime_high")
        s_scores, s_cmax, s_nmax, s_exp = sem("scores_summed"), sem("chunk_max"), sem("negmax"), sem("exp_done")
        s_pt, s_ptH, s_ptL = sem("prob_transposed"), sem("prob_high"), sem("prob_low")
        s_pv, s_och, s_o = sem("pv_summed"), sem("o_chain"), sem("o_normalized")
        s_oT, s_ao = sem("o_transposed"), sem("ao_summed")
        s_ct, s_ctH = sem("ctx_transposed"), sem("ctx_high")
        s_rowH, s_rowL = sem("rows_high"), sem("rows_low")
        s_misc = sem("misc_bank_free")
        s_t1, s_t2, s_t4, s_t5, s_t6 = (sem(n) for n in ("out_projected", "norms_transposed", "bc_projected",
                                                        "dt_projected", "y_projected"))
        s_var, s_rsq, s_norm = sem("variances"), sem("rsqrt_guess"), sem("x_normalized")
        s_tch, s_ach = sem("tail_dve_chain"), sem("tail_act_chain")
        s_bcst, s_sp, s_dt = sem("bc_stored"), sem("softplus_log"), sem("dt_ready")
        s_bcr = [sem("bc_group_loaded0"), sem("bc_group_loaded1")]
        s_dta, s_u, s_dA = sem("dta_ready"), sem("u_ready"), sem("decay_ready")
        s_scan, s_hc, s_red, s_y = sem("scan_done"), sem("hc_ready"), sem("slice_reduced"), sem("y_ready")
        s_fd, s_fa, s_fpe, s_fev = sem("ffn_dve"), sem("ffn_act"), sem("ffn_pe"), sem("ffn_copied")
        s_out = sem("out_stored")
        s_settled = sem("settled")
        s_dzero, s_dst, s_fwq, s_fq = sem("decay_zeroed"), sem("open_stats"), sem("ffn_weight_quantized"), sem("ffn_quantized")

        def tile_live(b, j, lag):
            return not isinstance(b, int) or 0 <= TILES * b + j - lag < NT

        def batch_live(b, lag):
            return not isinstance(b, int) or 0 <= b - lag < NB

        def misc_uses(b, j):
            return ([("q", tile_live(b, j, -1)), ("oT", tile_live(b, j, 3)), ("ctx", batch_live(b, -1)),
                     ("ao", tile_live(b, j, 3)), ("tail", batch_live(b, 1) and j in (2, 4, 5, 6)),
                     ("y", batch_live(b, 3) and j == 1)])

        def misc_in(b):
            return sum(bool(live) for j in range(TILES) for _, live in misc_uses(b, j))

        def misc_before(b, j, kind):
            n = 0
            if isinstance(b, int):
                n = sum(misc_in(i) for i in range(FIRST, b))
            else:
                n = (b - LOOP_FROM) * misc_in(LOOP_FROM) + sum(misc_in(i) for i in range(FIRST, LOOP_FROM))
            n += sum(bool(live) for i in range(j) for _, live in misc_uses(b, i))
            for k, live in misc_uses(b, j):
                if k == kind:
                    return n
                n += bool(live)

        def pipeline(eng, body):
            for b in range(FIRST, LOOP_FROM):
                body(b, b % 2)
            with eng.Fori(0, (LOOP_TO - LOOP_FROM) // 2) as i:
                body(2 * i + LOOP_FROM, LOOP_FROM % 2)
                body(2 * i + LOOP_FROM + 1, 1 - LOOP_FROM % 2)
            for b in range(LOOP_TO, LAST + 1):
                body(b, b % 2)

        def key_rows(kt):
            return P if kt < KT - 1 else KLAST

        def wait(eng, s, value):
            if not isinstance(value, int) or value > 0:
                eng.wait_ge(s, value)

        def settle(eng):
            eng.sem_inc(s_settled, 1)

        def half(par):
            return slice(NQ * par, NQ * par + NQ)

        def residual(b, par):
            v = x_rows[half(par)].rearrange("p r (c d) -> p (r c) d", c=2)
            if isinstance(b, int):
                return x_rows[half(par), b // 2, :]
            return v[:, bass.ds(b - par, 2), :].rearrange("p c d -> p (c d)")

        O_LN0 = 1 + 4 + 1
        TAIL_STEPS = 7
        F_VAR = 3
        xdT = bcr[1][:, 0, :].rearrange("p (r d) -> p r d", r=RT)

        OPEN_ACT, OPEN_DVE = 0, 1
        OPEN_BY = [k % 2 for k in range(8 + 3 + 2 + 8 + 1)]
        OPEN_BANKS = [[bank[0], bank[1]], [bank[2], bank[3]]]
        O_WK, O_XP, O_DTW, O_OP, O_X, O_Q, O_FW = 0, 8, 9, 10, 11, 13, 21

        def open_place(k):
            who = OPEN_BY[k]
            n = sum(w == who for w in OPEN_BY[:k])
            return who, n, OPEN_BANKS[who][n % 2]

        block = es.enter_context(nc.Block())

        @block.sync
        def _(sp):
            sp.dma_start(x_rows[:], x.rearrange("(r a) q d -> (a q) r d", a=2)).then_inc(s_x, 16)
            sp.dma_start(wk_a, Wk[0:P, :]).then_inc(s_wk, 16)
            sp.dma_start(wk_b, Wk[P:DC, :]).then_inc(s_wk, 16)
            sp.dma_start(wq_v[0], Wq[0:P, :]).then_inc(s_wq, 16)
            sp.dma_start(wq_v[1], Wq[P:2 * P, :]).then_inc(s_wq, 16)

            def load_raw(batch, g):
                k0, n = GROUPS[g]
                rest = key_rows(k0 + n - 1)
                dst = raw[g % 2][0:rest, 0:n, :]
                if isinstance(batch, int):
                    src = ctx[batch, k0 * P:k0 * P + (n - 1) * P + rest, :]
                else:
                    src = ctx[bass.ds(batch, 1), k0 * P:k0 * P + (n - 1) * P + rest, :].rearrange("o k d -> (o k) d")
                src = src.rearrange("(n p) d -> p n d", n=n)
                sp.dma_start(dst[:, :, 0:DC], src).then_inc(s_raw[g % 2], 16)
                sp.dma_start(dst[:, :, DC:], src[:, :, P:DC]).then_inc(s_raw[g % 2], 16)

            load_raw(0, 0)
            load_raw(0, 1)
            for dst, src in (
                (xp_bc, x_proj_w[RANK:RANK + 2 * STATE, :]), (xp_dt, x_proj_w[0:RANK, :]),
                (dtw_rows, dt_proj_w.rearrange("(h p) r -> p h r", h=2)),
                (op_rows, out_proj_w.rearrange("(h p) d -> p h d", h=2)),
                (fw_rows, ffn_w.rearrange("(h p) d -> p h d", h=2)),
                (negA[:], A_log.rearrange("(h p) n -> p h n", h=2)),
                (wv_a[:], Wv[0:P, :]), (wv_b[:], Wv[P:DC, :]),
                (wo[:], Wo.rearrange("(t p) d -> p t d", p=P)),
                (bias_r[:], ffn_b.partition_broadcast(P)), (bo_r[:], bo.partition_broadcast(P)),
            ):
                sp.dma_start(dst, src).then_inc(s_w, 16)
            with nc.allow_non_contiguous_dma(reason="256 values each, once"):
                for dst, src in ((norm_c, norm_w), (dtb_c, dt_proj_b), (D_c, D)):
                    sp.dma_start(dst, src.rearrange("(h p) -> p h", h=2)).then_inc(s_w, 16)

            for m in range(TILES):
                who, n, _ = open_place(O_Q + m)
                sp.wait_ge(s_oev[who], n + 1)
                sp.dma_start(q_scratch[:, :, m, :].rearrange("b p q -> p b q"),
                             q_stage[m % 2].rearrange("p (b q) -> p b q", b=NB)).then_inc(s_qst[m % 2], 16)
            for i in range(2):
                sp.wait_ge(s_qst[i], 16 * TILES // 2)
            sp.sem_inc(s_opened, 1)
            sp.wait_ge(s_opened, 5)

            def load_bc(batch, g):
                if isinstance(batch, int):
                    src = bc_scratch[batch]
                else:
                    src = bc_scratch[bass.ds(batch, 1)].rearrange("o s q -> (o s) q")
                src = src.rearrange("(w g n) q -> w g (n q)", w=2, g=SG)[:, g, :]
                sp.dma_start(bcr[g % 2][:], src.partition_broadcast(P)).then_inc(s_bcr[g % 2], 16)

            def body(b, par):
                if batch_live(b, -1):
                    nxt = 1 - par
                    wait(sp, s_qp, TILES * b)
                    settle(sp)
                    for h in range(2):
                        if isinstance(b, int):
                            src = q_scratch[b + 1, half(h)]
                        else:
                            src = q_scratch[bass.ds(b + 1, 1), half(h)].rearrange("o p t q -> (o p) t q")
                        sp.dma_start(qd[nxt][half(h), :, half(h)], src).then_inc(s_qd[nxt], 16)
                for j in range(TILES):
                    if batch_live(b, 2) and j == 0:
                        wait(sp, s_hc, SLICES * (b - 2))
                        settle(sp)
                        load_bc(b - 2, 1)
                    if batch_live(b, 2) and j in (2, 4):
                        sp.wait_ge(s_hc, SLICES * (b - 2) + j)
                        settle(sp)
                        load_bc(b - 2, j // 2 + 1)
                    if j % 2 == 1:
                        g = j // 2
                        nb, ng = (b + 1, g + 2) if g < 2 else (b + 2, g - 2)
                        if batch_live(b, -1):
                            sp.wait_ge(s_ct, 8 * (b + 1) + j + 1)
                            settle(sp)
                            sp.wait_ge(s_rowH, NG * (b + 1) + g + 1)
                            settle(sp)
                            sp.wait_ge(s_rowL, NG * (b + 1) + g + 1)
                            settle(sp)
                            if not isinstance(nb, int):
                                load_raw(nb % NB, ng)
                            elif nb < NB:
                                load_raw(nb, ng)
                    if batch_live(b, 1) and j == 6:
                        sp.wait_ge(s_misc, misc_before(b, 5, "tail") + 1)
                        settle(sp)
                        if isinstance(b, int):
                            dst = bc_scratch[b - 1]
                        else:
                            dst = bc_scratch[bass.ds(b - 1, 1)].rearrange("o s q -> (o s) q")
                        sp.dma_start(dst, bc[:]).then_inc(s_bcst, 16)
                    if batch_live(b, 1) and j == 7:
                        sp.wait_ge(s_bcst, 16 * b)
                        settle(sp)
                        wait(sp, s_hc, SLICES * (b - 1) - 2)
                        settle(sp)
                        load_bc(b - 1, 0)

            pipeline(sp, body)
            for r in range(RT):
                sp.wait_ge(s_fev, r + 1)
                sp.dma_start(out.rearrange("(r a) q d -> r (a q) d", a=2)[r], x_rows[:, r, :]).then_inc(s_out, 16)
            sp.wait_ge(s_out, 16 * RT)

        @block.gpsimd
        def _(pool):
            pool.memset(ident[:], 0.0).then_inc(s_id0, 1)
            pool.wait_ge(s_id0, 1)
            pool.affine_select(out=ident[:], in_=ident[:], compare_op=ALU.not_equal, fill=1.0, base=0,
                               pattern=[[-1, P]], channel_multiplier=1).then_inc(s_ident, 1)
            pool.memset(one_c[:], 1.0)
            for i in range(2):
                pool.memset(qd[i][:], 0.0)
                pool.memset(rows[i][:, :, DC:DC + 1].bitcast(F32), 1.0)
                pool.memset(rows[i][:, :, DC + 1:RH].bitcast(F32), 0.0)
                pool.memset(ctH[i][:, NK:NKP].bitcast(F32), 0.0)
                pool.memset(ctL[i][:, NK:NKP].bitcast(F32), 0.0)
                pool.memset(ctT[i][:, NK:NKP].bitcast(F32), 0.0)
                pool.memset(qpL[i][:].bitcast(F32), 0.0)
            pool.memset(zdt[:], 0.0).then_inc(s_opened, 1)
            pool.wait_ge(s_opened, 5)
            for i in range(2):
                last = pool.memset(dA[i][:, :, 0:1], 0.0)
            last.then_inc(s_dzero, 1)

            def hc(batch, s):
                k = SLICES * batch + s
                g = s // 2
                pool.wait_ge(s_scan, k + 1)
                pool.tensor_tensor(hs[s % 2][:], hs[s % 2][:],
                                   bcr[g % 2][:, 1, :].rearrange("p (n q) -> p n q", n=NS), ALU.mult).then_inc(s_hc, 1)

            def prepare(batch, par, s):
                k = SLICES * batch + s
                g, h = s // 2, s % 2
                wait(pool, s_scan, k - 1)
                pool.tensor_tensor(dA[s % 2][:, :, 1:NQ],
                                   dt_[par][:, h, 1:NQ].unsqueeze(1).broadcast_to([P, NS, NQ - 1]),
                                   negA[:, h, NS * g:NS * g + NS].unsqueeze(2).broadcast_to([P, NS, NQ - 1]),
                                   ALU.mult).then_inc(s_dta, 1)
                wait(pool, s_red, k - 1)
                pool.wait_ge(s_bcr[g % 2], 16 * (2 * batch + g // 2 + 1))
                pool.tensor_tensor(hs[s % 2][:],
                                   dtx[par][:, h, :].unsqueeze(1).broadcast_to([P, NS, NQ]),
                                   bcr[g % 2][:, 0, :].rearrange("p (n q) -> p n q", n=NS), ALU.mult).then_inc(s_u, 1)

            def body(b, par):
                for j in range(TILES):
                    if batch_live(b, 3) and j == 0:
                        hc(b - 3, SLICES - 1)
                    if batch_live(b, 2):
                        if j == 0:
                            pool.wait_ge(s_dt, b - 1)
                            prepare(b - 2, par, 0)
                        else:
                            hc(b - 2, j - 1)
                        if j + 1 < SLICES:
                            prepare(b - 2, par, j + 1)
                    if batch_live(b, -1) and j % 2 == 1:
                        g = j // 2
                        k0, n = GROUPS[g]
                        rest = key_rows(k0 + n - 1)
                        nxt = 1 - par
                        pool.wait_ge(s_rowH, NG * (b + 1) + g + 1)
                        pool.tensor_tensor(rows[nxt][0:rest, k0:k0 + n, RH:RW], raw[g % 2][0:rest, 0:n, 0:DC],
                                           rows[nxt][0:rest, k0:k0 + n, 0:DC].bitcast(F32),
                                           ALU.subtract).then_inc(s_rowL, 1)

            pipeline(pool, body)

        @block.scalar
        def _(act):
            step = [0]

            def link(ins, s=s_oact):
                step[0] += 1
                ins.then_inc(s, 1)
                act.wait_ge(s, step[0])

            def open_copy(k, dst, shape=None, scale=1.0):
                who, n, bk = open_place(k)
                act.wait_ge(s_ope[who], n + 1)
                act.activation(dst, shape(bk), ACT.Copy, scale=scale).then_inc(s_oev[who], 1)

            act.wait_ge(s_odve, 1)
            link(act.activation(rs0[:], ve[:], ACT.Ln))
            link(act.activation(rs1[:], rs0[:], ACT.Exp, scale=-0.5))
            act.wait_ge(s_w, 16 * 14)
            link(act.activation(negA[:], negA[:], ACT.Exp))
            for m in range(0, TILES, 2):
                open_copy(O_WK + m, wkT[:, m, :], lambda bk: bk[:, 0:DC])
            open_copy(O_XP, xpT[:], lambda bk: bk[:, 0:2 * (RANK + 2 * STATE)].rearrange("p (h n) -> p h n", h=2))
            open_copy(O_OP, opT[:], lambda bk: bk[:].rearrange("p (h n) -> p h n", h=2))
            open_copy(O_X + 1, xT0[:, 1, :], lambda bk: bk[:])
            for m in range(1, TILES, 2):
                if m >= 2:
                    act.wait_ge(s_qst[m % 2], 16 * (m // 2))
                open_copy(O_Q + m, q_stage[m % 2], lambda bk: bk[:], scale=DH ** -0.5)
            act.wait_ge(s_oev[OPEN_ACT], sum(w == OPEN_ACT for w in OPEN_BY))
            act.sem_inc(s_opened, 1)
            act.wait_ge(s_opened, 5)

            def high_of_group(t, g):
                k0, n = GROUPS[g]
                m = key_rows(k0 + n - 1)
                act.wait_ge(s_pt, NG * t + g + 1)
                wait(act, s_pv, NG * t + g - 1)
                act.activation(ptH[g % 2][0:m, 0:n, :], pt_bank[g % 2][0:m, 0:n * P].rearrange("p (n q) -> p n q", n=n),
                               ACT.Copy).then_inc(s_ptH, 1)

            def exp_of_chunk(t, c):
                c0, n = CHUNKS[c]
                act.wait_ge(s_nmax, t + 1)
                wait(act, s_pt, NG * (t - 1) + c + 1)
                act.activation(prob[:, c0:c0 + n], bank[c][:, 0:n], ACT.Exp, bias=nmax[:, 0:1]).then_inc(s_exp, 1)

            def body(b, par):
                nxt = 1 - par
                B = b - 1
                for j in range(TILES):
                    t = TILES * b + j
                    if tile_live(b, j, -1):
                        i = (j + 1) % 2
                        act.wait_ge(s_qp, t + 2)
                        act.activation(qpH[i][:].rearrange("p a q -> p (a q)"), misc[:, 0:2 * P], ACT.Copy).then_inc(s_qpH, 1)
                    if tile_live(b, j, 1):
                        exp_of_chunk(t - 1, 1)
                        exp_of_chunk(t - 1, 2)
                        high_of_group(t - 1, 0)
                    if tile_live(b, j, 3):
                        act.wait_ge(s_oT, t - 2)
                        act.activation(oT[:, 0, :], misc[:, 0:P], ACT.Copy)
                        act.activation(oT[0:DT, 1, :], misc[0:DT, P:2 * P], ACT.Copy).then_inc(s_misc, 1)
                    if tile_live(b, j, 1):
                        exp_of_chunk(t - 1, 3)
                        high_of_group(t - 1, 1)
                    if batch_live(b, -1):
                        g = j // 2
                        k0, n = GROUPS[g]
                        w = min(n * P, NK - k0 * P)
                        dst = (ctH, ctT)[j % 2][nxt]
                        act.wait_ge(s_ct, 8 * (b + 1) + j + 1)
                        act.activation(dst[:, k0 * P:k0 * P + w], misc[:, 0:w], ACT.Copy).then_inc(s_ctH, 1)
                    if batch_live(b, 2):
                        for s in ((0, 1) if j == 0 else (j + 1,)):
                            if s < SLICES:
                                act.wait_ge(s_dta, SLICES * (b - 2) + s + 1)
                                act.activation(dA[s % 2][:, :, 1:NQ], dA[s % 2][:, :, 1:NQ], ACT.Exp).then_inc(s_dA, 1)
                    if batch_live(b, 1) and j == 3:
                        act.wait_ge(s_var, b)
                        act.activation(rs0[half(nxt), 0:2], ve[half(nxt), 0:2], ACT.Ln).then_inc(s_ach, 1)
                        act.wait_ge(s_ach, 2 * B + 1)
                        act.activation(rs1[half(nxt), 0:2], rs0[half(nxt), 0:2], ACT.Exp, scale=-0.5).then_inc(s_rsq, 1)
                    if batch_live(b, -1) and j % 2 == 1:
                        g = j // 2
                        k0, n = GROUPS[g]
                        rest = key_rows(k0 + n - 1)
                        act.wait_ge(s_raw[g % 2], 32 * (2 * (b + 1) + g // 2 + 1))
                        wait(act, s_pv, NG * TILES * b)
                        act.activation(rows[nxt][0:rest, k0:k0 + n, 0:DC], raw[g % 2][0:rest, 0:n, 0:DC], ACT.Copy).then_inc(s_rowH, 1)
                    if tile_live(b, j, 1):
                        high_of_group(t - 1, 2)
                    if tile_live(b, j, 3):
                        act.wait_ge(s_ao, t - 2)
                        tl = (j - 3) % TILES
                        act.activation(ao[par if j >= 3 else nxt][:, tl, :], misc[:, 0:NQ], ACT.Copy).then_inc(s_misc, 1)
                    if tile_live(b, j, 1):
                        high_of_group(t - 1, 3)
                    if batch_live(b, 1) and j == 4:
                        act.wait_ge(s_t2, b)
                        for h in range(2):
                            act.activation(ypart[nxt][:, h, SG, :], misc[:, NQ * h:NQ * h + NQ], ACT.Copy, scale=D_c[:, h:h + 1])
                            last = act.activation(xnT[:, h, :], misc[:, NQ * (2 + h):NQ * (3 + h)], ACT.Copy,
                                                  scale=norm_c[:, h:h + 1])
                        last.then_inc(s_misc, 1)
                    if batch_live(b, 1) and j == 5:
                        act.wait_ge(s_t4, b)
                        wait(act, s_bcst, 16 * B)
                        act.activation(bc[:], misc[:, 0:NQ], ACT.Copy)
                        act.activation(dlo[:], misc[0:RANK, NQ:2 * NQ], ACT.Copy).then_inc(s_misc, 1)
                    if batch_live(b, 1) and j == 6:
                        act.wait_ge(s_t5, b)
                        wait(act, s_dt, B)
                        for h in range(2):
                            last = act.activation(zdt[:, h, :], misc[:, NQ * h:NQ * h + NQ], ACT.Identity,
                                                  bias=dtb_c[:, h:h + 1])
                        last.then_inc(s_misc, 1)
                    if tile_live(b, j, 0):
                        exp_of_chunk(t, 0)
                    if batch_live(b, 1) and j == 6:
                        act.wait_ge(s_misc, misc_before(b, j, "tail") + 1)
                        act.activation(sp1[:], zdt[:], ACT.Abs).then_inc(s_ach, 1)
                        act.wait_ge(s_ach, 2 * b)
                        act.activation(sp1[:], sp1[:], ACT.Exp, scale=-1.0).then_inc(s_sp, 1)
                        act.wait_ge(s_sp, 2 * B + 1)
                        act.activation(sp1[:], sp1[:], ACT.Ln, bias=one_c[:]).then_inc(s_sp, 1)

            pipeline(act, body)

            act.wait_ge(s_fd, F_VAR)
            act.activation(rs0[:], ve[:], ACT.Ln).then_inc(s_fa, 1)
            act.wait_ge(s_fa, 1)
            act.activation(rs1[:], rs0[:], ACT.Exp, scale=-0.5).then_inc(s_fa, 1)
            for r in range(RT):
                act.wait_ge(s_fpe, 2 * r + 1)
                act.activation(xdT[:, r, :], bank[r % 2][:, 0:DM], ACT.Copy).then_inc(s_fa, 1)

        @block.vector
        def _(dve):
            step = [0]

            def link(ins):
                step[0] += 1
                ins.then_inc(s_odve, 1)
                dve.wait_ge(s_odve, step[0])

            def open_copy(k, dst, shape, scale=None):
                who, n, bk = open_place(k)
                dve.wait_ge(s_ope[who], n + 1)
                if scale is None:
                    dve.tensor_copy(dst, shape(bk)).then_inc(s_oev[who], 1)
                else:
                    dve.tensor_scalar(dst, shape(bk), scale, None, ALU.mult).then_inc(s_oev[who], 1)

            def newton(link, r1, r0, v):
                link(dve.tensor_tensor(r0, r1, r1, ALU.mult))
                link(dve.tensor_tensor(r0, r0, v, ALU.mult))
                link(dve.tensor_scalar(r0, r0, -0.5, 1.5, ALU.mult, ALU.add))
                link(dve.tensor_tensor(r0, r0, r1, ALU.mult))

            def layernorm_stats(link, src):
                for r in range(RT):
                    last = dve.bn_stats(st[:, r, :], src[:, r, :])
                link(last)
                for r in range(RT):
                    last = dve.bn_aggr(mv[:, r, :], st[:, r, :])
                link(last)

            def mx_quantize(link, v, tmp, scale, inv):
                a, b, c, d = tmp
                vb, ab, db = (m.rearrange("p (k e) -> p k e", e=FP6_BLOCK) for m in (v, a, d))
                link(dve.tensor_reduce(scale, vb, AX.X, ALU.max, apply_absolute_value=True))
                link(dve.tensor_scalar(scale, scale, 1.0 / FP6_MAX, SCALE_FLOOR, ALU.mult, ALU.max))
                link(dve.reciprocal(inv, scale))
                shape = list(vb.shape)
                link(dve.tensor_tensor(ab, vb, inv.unsqueeze(2).broadcast_to(shape), ALU.mult))
                link(dve.tensor_tensor(b, a, a, ALU.mult))
                link(dve.tensor_scalar(c, b, 16.0, None, ALU.is_ge))
                link(dve.tensor_scalar(b, b, 4.0, None, ALU.is_ge))
                link(dve.tensor_scalar(d, c, -2.0, 8.0, ALU.mult, ALU.add))
                link(dve.scalar_tensor_tensor(d, b, -4.0, d, ALU.mult, ALU.add))
                link(dve.tensor_tensor(a, a, d, ALU.mult))
                link(dve.tensor_scalar(d, a, ROUND, ROUND, ALU.add, ALU.subtract))
                link(dve.tensor_tensor(a, d, a, ALU.subtract))
                link(dve.scalar_tensor_tensor(d, a, 0.5, d, ALU.is_ge, ALU.subtract))
                link(dve.tensor_scalar(b, b, -0.125, -0.125, ALU.mult, ALU.add))
                link(dve.scalar_tensor_tensor(b, c, 1.0, b, ALU.add, ALU.mult))
                link(dve.tensor_tensor(d, d, b, ALU.mult))
                link(dve.tensor_tensor(vb, db, scale.unsqueeze(2).broadcast_to(shape), ALU.mult))

            dve.wait_ge(s_x, 16)
            for r in range(RT):
                last = dve.bn_stats(st[:, r, :], x_rows[:, r, :])
            last.then_inc(s_dst, 1)
            dve.wait_ge(s_dst, 1)
            for r in range(RT):
                last = dve.bn_aggr(mv[:, r, :], st[:, r, :])
            last.then_inc(s_dst, 1)
            dve.wait_ge(s_dst, 2)
            link(dve.tensor_scalar(ve[:], mv[:, :, 1], LN_EPS, None, ALU.add))
            dve.wait_ge(s_oact, 2)
            newton(link, rs1[:], rs0[:], ve[:])
            for r in range(RT):
                last = dve.tensor_scalar(x0[:, r, :], x_rows[:, r, :], mv[:, r, 0:1], rs0[:, r:r + 1],
                                         ALU.subtract, ALU.mult)
            link(last)
            dve.wait_ge(s_w, 16 * 14)
            link(dve.tensor_tensor(x_rows[:], x_rows[:], bo_r[:].unsqueeze(1).broadcast_to([P, RT, DM]), ALU.add))
            for m in range(1, TILES, 2):
                open_copy(O_WK + m, wkT[:, m, :], lambda bk: bk[:, 0:DC])
            open_copy(O_DTW, dtwT[:], lambda bk: bk[0:RANK, 0:DM])
            open_copy(O_X, xT0[:, 0, :], lambda bk: bk[:])
            for m in range(0, TILES, 2):
                if m >= 2:
                    dve.wait_ge(s_qst[m % 2], 16 * (m // 2))
                open_copy(O_Q + m, q_stage[m % 2], lambda bk: bk[:], scale=DH ** -0.5)
            dve.wait_ge(s_oact, 3)
            link(dve.tensor_scalar(negA[:], negA[:], -1.0, None, ALU.mult))
            n = 2 * DM
            fw = fw_rows.rearrange("p h d -> p (h d)")
            mx_quantize(link, fw, [prob[:, 0:n], prob[:, n:2 * n], prob[:, 2 * n:3 * n], flat(ao[0])],
                        olow[:, 0:n // FP6_BLOCK], olow[:, 64:64 + n // FP6_BLOCK])
            dve.sem_inc(s_fwq, 1)
            open_copy(O_FW, wdT[:], lambda bk: bk[:].rearrange("p (h n) -> p h n", h=2))
            dve.wait_ge(s_oev[OPEN_DVE], sum(w == OPEN_DVE for w in OPEN_BY))
            dve.sem_inc(s_opened, 1)
            dve.wait_ge(s_opened, 5)

            def low_of_group(t, g):
                k0, n = GROUPS[g]
                m = key_rows(k0 + n - 1)
                dve.wait_ge(s_ptH, NG * t + g + 1)
                dve.tensor_tensor(ptL[g % 2][0:m, 0:n, :], pt_bank[g % 2][0:m, 0:n * P].rearrange("p (n q) -> p n q", n=n),
                                  ptH[g % 2][0:m, 0:n, :].bitcast(F32), ALU.subtract).then_inc(s_ptL, 1)

            def chunk_max(t, c):
                _, n = CHUNKS[c]
                dve.wait_ge(s_scores, NG * t + c + 1)
                dve.tensor_reduce(cmax[:, c:c + 1], bank[c][:, 0:n], AX.X, ALU.max).then_inc(s_cmax, 1)

            def reduce_slice(batch, par, s):
                dve.wait_ge(s_hc, SLICES * batch + s + 1)
                dve.tensor_reduce(ypart[par][:, s % 2, s // 2, :], hs[s % 2][:].rearrange("p n q -> p q n"),
                                  AX.X, ALU.add).then_inc(s_red, 1)

            def body(b, par):
                nxt = 1 - par
                B = b - 1
                for j in range(TILES):
                    t = TILES * b + j
                    if tile_live(b, j, -1):
                        i = (j + 1) % 2
                        dve.wait_ge(s_qpH, t + 2)
                        dve.tensor_tensor(qpL[i][:].rearrange("p a q -> p (a q)"), misc[:, 0:2 * P],
                                          qpH[i][:].rearrange("p a q -> p (a q)").bitcast(F32), ALU.subtract).then_inc(s_misc, 1)
                    if tile_live(b, j, 0):
                        chunk_max(t, 0)
                    if tile_live(b, j, 2):
                        dve.wait_ge(s_pv, NG * (t - 1))
                        dve.reciprocal(rinv[:], o_bank[:, DC:DC + 1]).then_inc(s_och, 1)
                        dve.wait_ge(s_och, 2 * (t - 2) + 1)
                        dve.tensor_scalar(olow[:], o_bank[:, RH:RW], rinv[:], None, ALU.mult).then_inc(s_och, 1)
                        dve.wait_ge(s_och, 2 * (t - 2) + 2)
                        wait(dve, s_oT, t - 3)
                        dve.scalar_tensor_tensor(osb[j % 2][:], o_bank[:, 0:DC], rinv[:], olow[:],
                                                 ALU.mult, ALU.add).then_inc(s_o, 1)
                    if tile_live(b, j, 1):
                        low_of_group(t - 1, 0)
                    if tile_live(b, j, 0):
                        chunk_max(t, 1)
                    if batch_live(b, 3) and j == 0:
                        reduce_slice(b - 3, nxt, SLICES - 1)
                        dve.wait_ge(s_red, SLICES * (b - 2))
                        dve.tensor_reduce(yT[:], ypart[nxt][:].rearrange("p h g q -> p h q g"), AX.X, ALU.add).then_inc(s_y, 1)
                    if batch_live(b, 2) and j >= 1:
                        reduce_slice(b - 2, par, j - 1)
                    if tile_live(b, j, 1):
                        low_of_group(t - 1, 1)
                    if batch_live(b, -1):
                        g = j // 2
                        k0, n = GROUPS[g]
                        w = min(n * P, NK - k0 * P)
                        dve.wait_ge(s_ctH, 8 * (b + 1) + j + 1)
                        if j % 2 == 0:
                            dve.tensor_tensor(ctL[nxt][:, k0 * P:k0 * P + w], misc[:, 0:w],
                                              ctH[nxt][:, k0 * P:k0 * P + w].bitcast(F32), ALU.subtract).then_inc(s_misc, 1)
                        else:
                            v = ctT[nxt][DT:P, k0 * P:k0 * P + w]
                            dve.tensor_tensor(v, misc[DT:P, 0:w], v.bitcast(F32), ALU.subtract).then_inc(s_misc, 1)
                    if tile_live(b, j, 0):
                        chunk_max(t, 2)
                    if tile_live(b, j, 1):
                        low_of_group(t - 1, 2)
                    if tile_live(b, j, 0):
                        chunk_max(t, 3)
                        dve.wait_ge(s_cmax, NG * (t + 1))
                        wait(dve, s_exp, NG * t)
                        dve.tensor_reduce(nmax[:, 0:1], cmax[:], AX.X, ALU.max, negate=True).then_inc(s_nmax, 1)
                    if tile_live(b, j, 1):
                        low_of_group(t - 1, 3)
                    if batch_live(b, 3) and j == 1:
                        dve.wait_ge(s_t6, b - 2)
                        r = residual(b - 3, nxt)
                        dve.tensor_tensor(r, misc[half(nxt), 0:DM], r, ALU.add).then_inc(s_misc, 1)
                    if batch_live(b, 1) and j == 2:
                        h = half(nxt)
                        r = residual(B, nxt)
                        dve.wait_ge(s_t1, b)
                        dve.tensor_tensor(r, misc[h, 0:DM], r, ALU.add).then_inc(s_misc, 1)
                        dve.wait_ge(s_misc, misc_before(b, j, "tail") + 1)
                        k = TAIL_STEPS * B
                        settle(dve)
                        dve.bn_stats(st[h, 0, :], r).then_inc(s_tch, 1)
                        dve.wait_ge(s_tch, k + 1)
                        settle(dve)
                        dve.bn_aggr(mv[h, 0, :], st[h, 0, :]).then_inc(s_tch, 1)
                        dve.wait_ge(s_tch, k + 2)
                        dve.tensor_scalar(ve[h, 0:1], mv[h, 0, 1:2], LN_EPS, None, ALU.add)
                        dve.tensor_scalar(ve[h, 1:2], mv[h, 0, 1:2], 1.0 + RMS_EPS, RMS_EPS * LN_EPS,
                                          ALU.mult, ALU.add).then_inc(s_var, 1)
                    if batch_live(b, 2):
                        s = j
                        k = SLICES * (b - 2) + s
                        dve.wait_ge(s_dA, k + 1)
                        dve.wait_ge(s_u, k + 1)
                        hflat = hs[s % 2][:].rearrange("p n q -> p (n q)")
                        dve.tensor_tensor_scan(out=hflat, data0=dA[s % 2][:].rearrange("p n q -> p (n q)"), data1=hflat,
                                               initial=0.0, op0=ALU.mult, op1=ALU.add).then_inc(s_scan, 1)
                    if batch_live(b, 1) and j == 3:
                        h = half(nxt)
                        r = residual(B, nxt)
                        k = TAIL_STEPS * B + 2
                        dve.wait_ge(s_rsq, b)
                        dve.tensor_tensor(rs0[h, 0:2], rs1[h, 0:2], rs1[h, 0:2], ALU.mult).then_inc(s_tch, 1)
                        dve.wait_ge(s_tch, k + 1)
                        dve.tensor_tensor(rs0[h, 0:2], rs0[h, 0:2], ve[h, 0:2], ALU.mult).then_inc(s_tch, 1)
                        dve.wait_ge(s_tch, k + 2)
                        dve.tensor_scalar(rs0[h, 0:2], rs0[h, 0:2], -0.5, 1.5, ALU.mult, ALU.add).then_inc(s_tch, 1)
                        dve.wait_ge(s_tch, k + 3)
                        dve.tensor_tensor(rs0[h, 0:2], rs0[h, 0:2], rs1[h, 0:2], ALU.mult).then_inc(s_tch, 1)
                        dve.wait_ge(s_tch, k + 4)
                        for i in range(2):
                            last = dve.tensor_scalar(xln[h, i, :], r, mv[h, 0, 0:1], rs0[h, i:i + 1], ALU.subtract, ALU.mult)
                        last.then_inc(s_norm, 1)
                    if batch_live(b, 1) and j == 7:
                        dve.wait_ge(s_sp, 2 * b)
                        dve.scalar_tensor_tensor(dt_[nxt][:], zdt[:], 0.0, sp1[:], ALU.max, ALU.add).then_inc(s_tch, 1)
                        dve.wait_ge(s_tch, TAIL_STEPS * b)
                        dve.tensor_tensor(dtx[nxt][:], dt_[nxt][:], xnT[:], ALU.mult).then_inc(s_dt, 1)

            pipeline(dve, body)

            count = [0]

            def flink(ins):
                count[0] += 1
                ins.then_inc(s_fd, 1)
                dve.wait_ge(s_fd, count[0])

            dve.wait_ge(s_misc, misc_before(LAST + 1, 0, "q"))
            layernorm_stats(flink, x_rows)
            flink(dve.tensor_scalar(ve[:], mv[:, :, 1], LN_EPS, None, ALU.add))
            assert count[0] == F_VAR
            dve.wait_ge(s_fa, 2)
            newton(flink, rs1[:], rs0[:], ve[:])
            v = flat(dA[0]).rearrange("p (r d) -> p r d", r=RT)
            for r in range(RT):
                last = dve.tensor_scalar(v[:, r, :], x_rows[:, r, :], mv[:, r, 0:1], rs0[:, r:r + 1], ALU.subtract, ALU.mult)
            flink(last)
            flink(dve.tensor_tensor(x_rows[:], x_rows[:], bias_r[:].unsqueeze(1).broadcast_to([P, RT, DM]), ALU.add))
            mx_quantize(flink, flat(dA[0]), [flat(dA[1]), flat(hs[0]), flat(hs[1]), bcr[0][:, 0, :]],
                        olow[:, 0:RT * DM // FP6_BLOCK], olow[:, 64:64 + RT * DM // FP6_BLOCK])
            dve.sem_inc(s_fq, 1)
            for r in range(RT):
                dve.wait_ge(s_fpe, 2 * r + 2)
                dve.tensor_tensor(x_rows[:, r, :], bank[2 + r % 2][:, 0:DM], x_rows[:, r, :], ALU.add).then_inc(s_fev, 1)

        @block.tensor
        def _(pe):
            def open_use(k):
                who, n, bk = open_place(k)
                wait(pe, s_oev[who], n - 1)
                return s_ope[who], bk

            pe.wait_ge(s_ident, 1)
            pe.wait_ge(s_wk, 32)
            for m in range(TILES):
                done, bk = open_use(O_WK + m)
                pe.transpose(bk[:, 0:P], wk_a[:, m * P:m * P + P], ident[:])
                pe.transpose(bk[:, P:DC], wk_b[:, m * P:m * P + P], ident[0:DT, 0:DT]).then_inc(done, 1)
            pe.wait_ge(s_w, 16 * 14)
            done, bk = open_use(O_XP)
            XP = RANK + 2 * STATE
            for h in range(2):
                pe.transpose(bk[:, XP * h:XP * h + RANK], xp_dt[:, P * h:P * h + P], ident[0:RANK, 0:RANK])
                last = pe.transpose(bk[:, XP * h + RANK:XP * h + XP], xp_bc[:, P * h:P * h + P], ident[:])
            last.then_inc(done, 1)
            done, bk = open_use(O_DTW)
            for h in range(2):
                last = pe.transpose(bk[0:RANK, P * h:P * h + P], dtw_rows[:, h, :], ident[:])
            last.then_inc(done, 1)

            def transpose_square(k, src):
                done, bk = open_use(k)
                for h in range(2):
                    for o in range(2):
                        last = pe.transpose(bk[:, DM * h + P * o:DM * h + P * o + P], src[:, o, P * h:P * h + P], ident[:])
                last.then_inc(done, 1)

            transpose_square(O_OP, op_rows)
            pe.wait_ge(s_odve, O_LN0)
            for h in range(2):
                done, bk = open_use(O_X + h)
                for r in range(RT):
                    last = pe.transpose(bk[:, P * r:P * r + P], x0[:, r, P * h:P * h + P], ident[:])
                last.then_inc(done, 1)
            for who, n in ((open_place(O_X)[0], open_place(O_X)[1]), (open_place(O_X + 1)[0], open_place(O_X + 1)[1])):
                pe.wait_ge(s_oev[who], n + 1)
            pe.wait_ge(s_wq, 32)
            for m in range(TILES):
                done, bk = open_use(O_Q + m)
                pe.matmul(bk[:], wq_v[0][:, m * P:m * P + P], xT0[:, 0, :], start=True, stop=False)
                pe.matmul(bk[:], wq_v[1][:, m * P:m * P + P], xT0[:, 1, :], start=False, stop=True).then_inc(done, 1)
            pe.wait_ge(s_fwq, 1)
            transpose_square(O_FW, fw_rows)
            for who in range(2):
                pe.wait_ge(s_oev[who], sum(w == who for w in OPEN_BY))
            pe.sem_inc(s_opened, 1)
            pe.wait_ge(s_opened, 5)

            def transpose_group(t, g):
                k0, n = GROUPS[g]
                pe.wait_ge(s_exp, NG * t + g + 1)
                wait(pe, s_ptL, NG * t + g - 1)
                for k in range(n):
                    m = key_rows(k0 + k)
                    last = pe.transpose(pt_bank[g % 2][0:m, k * P:k * P + P], prob[:, (k0 + k) * P:(k0 + k) * P + m], ident[:])
                last.then_inc(s_pt, 1)

            def pv_group(t, g, ctx_rows):
                k0, n = GROUPS[g]
                pe.wait_ge(s_ptL, NG * t + g + 1)
                if g == 0:
                    wait(pe, s_o, t)
                for k in range(n):
                    m = key_rows(k0 + k)
                    pe.matmul(o_bank[:, 0:RW], ptH[g % 2][0:m, k, :], ctx_rows[0:m, k0 + k, :],
                              start=k0 + k == 0, stop=False)
                    last = pe.matmul(o_bank[:, 0:RH], ptL[g % 2][0:m, k, :], ctx_rows[0:m, k0 + k, 0:RH],
                                     start=False, stop=k0 + k == KT - 1)
                last.then_inc(s_pv, 1)

            def scores(t, i, par, c):
                c0, n = CHUNKS[c]
                n += n % 2
                wait(pe, s_exp, NG * (t - 1) + c + 1)
                o = bank[c][:, 0:n]
                keys = slice(c0, c0 + n)
                pe.matmul(o, qpH[i][:, 0, :], ctH[par][:, keys], start=True, stop=False)
                pe.matmul(o, qpH[i][:, 0, :], ctL[par][:, keys], start=False, stop=False)
                pe.matmul(o, qpL[i][:, 0, :], ctH[par][:, keys], start=False, stop=False)
                pe.matmul(o, qpH[i][:, 1, :], ctT[par][:, keys], start=False, stop=False)
                pe.matmul(o, qpL[i][:, 1, :], ctT[par][:, keys], start=False, stop=True).then_inc(s_scores, 1)

            def body(b, par):
                nxt = 1 - par
                B = b - 1
                for j in range(TILES):
                    t = TILES * b + j
                    tl = (j - 3) % TILES
                    if tile_live(b, j, -1) or tile_live(b, j, 0):
                        wait(pe, s_misc, misc_before(b, j, "q"))
                    if tile_live(b, j, -1):
                        i = (j + 1) % TILES
                        qb = qd[par if j < TILES - 1 else nxt]
                        if j == TILES - 1:
                            if par == 0:
                                pe.wait_ge(s_qd[1], 16 * (b + 2))
                            else:
                                pe.wait_ge(s_qd[0], 16 * (b + 3))
                        pe.matmul(misc[:, 0:P], wkT[:, i, 0:P], qb[:, i, :], start=True, stop=True)
                        tail_w = wkT[:, i, P:DC]
                        pe.matmul(misc[0:DT, P:2 * P], tail_w, qb[:, i, :], start=True, stop=True)
                        pe.matmul(misc[DT:P, P:2 * P], tail_w, qb[:, i, :], start=True, stop=True).then_inc(s_qp, 1)
                    if tile_live(b, j, 0):
                        scores(t, j % 2, par, 0)
                    if tile_live(b, j, 1):
                        transpose_group(t - 1, 0)
                    if tile_live(b, j, 3):
                        wait(pe, s_misc, misc_before(b, j, "oT"))
                        pe.wait_ge(s_o, t - 2)
                        pe.transpose(misc[:, 0:P], osb[(j + 1) % 2][:, 0:P], ident[:])
                        pe.transpose(misc[0:DT, P:2 * P], osb[(j + 1) % 2][:, P:DC], ident[:]).then_inc(s_oT, 1)
                    if tile_live(b, j, 0):
                        scores(t, j % 2, par, 1)
                    if tile_live(b, j, 1):
                        transpose_group(t - 1, 1)
                    if batch_live(b, -1):
                        g = j // 2
                        k0, n = GROUPS[g]
                        wait(pe, s_misc, misc_before(b, j, "ctx"))
                        pe.wait_ge(s_raw[g % 2], 32 * (2 * (b + 1) + g // 2 + 1))
                        for k in range(n):
                            m = key_rows(k0 + k)
                            if j % 2 == 0:
                                src = raw[g % 2][0:m, k, 0:P]
                            else:
                                src = raw[g % 2][0:m, k, P:]
                            last = pe.transpose(misc[:, k * P:k * P + m], src, ident[0:m, 0:m])
                        last.then_inc(s_ct, 1)
                    pv_rows = rows[par if j else nxt]
                    if tile_live(b, j, 1) and j == 1:
                        pe.wait_ge(s_rowL, NG * (b + 1))
                    if tile_live(b, j, 1):
                        pv_group(t - 1, 0, pv_rows)
                    if tile_live(b, j, 0):
                        scores(t, j % 2, par, 2)
                    if tile_live(b, j, 1):
                        transpose_group(t - 1, 2)
                    if tile_live(b, j, 3):
                        wait(pe, s_misc, misc_before(b, j, "ao"))
                        for h in range(2):
                            q = slice(NQ * h, NQ * h + NQ)
                            c = tl * P + DH * h
                            pe.matmul(misc[q, 0:NQ], wv_a[:, c:c + DH], oT[:, 0, q], start=True, stop=False)
                            last = pe.matmul(misc[q, 0:NQ], wv_b[:, c:c + DH], oT[0:DT, 1, q], start=False, stop=True)
                        last.then_inc(s_ao, 1)
                    if tile_live(b, j, 1):
                        pv_group(t - 1, 1, pv_rows)
                    if tile_live(b, j, 0):
                        scores(t, j % 2, par, 3)
                    if tile_live(b, j, 1):
                        transpose_group(t - 1, 3)
                    if batch_live(b, 1) and j == 2:
                        pe.wait_ge(s_misc, misc_before(b, j, "tail"))
                        for m in range(TILES):
                            last = pe.matmul(misc[half(nxt), 0:DM], ao[nxt][:, m, :], wo[:, m, :],
                                             start=m == 0, stop=m == TILES - 1)
                        last.then_inc(s_t1, 1)
                    if batch_live(b, 1) and j == 4:
                        pe.wait_ge(s_misc, misc_before(b, j, "tail"))
                        pe.wait_ge(s_norm, b)
                        settle(pe)
                        h0 = half(nxt)
                        for i in range(4):
                            last = pe.transpose(misc[:, NQ * i:NQ * i + NQ], xln[h0, i // 2, P * (i % 2):P * (i % 2) + P],
                                                ident[h0, h0])
                        last.then_inc(s_t2, 1)
                    if batch_live(b, 1) and j == 5:
                        pe.wait_ge(s_misc, misc_before(b, j, "tail"))
                        for h in range(2):
                            pe.matmul(misc[:, 0:NQ], xpT[:, h, RANK:], xnT[:, h, :], start=h == 0, stop=h == 1)
                        for h in range(2):
                            last = pe.matmul(misc[0:RANK, NQ:2 * NQ], xpT[:, h, 0:RANK], xnT[:, h, :], start=h == 0, stop=h == 1)
                        last.then_inc(s_t4, 1)
                    if batch_live(b, 1) and j == 6:
                        pe.wait_ge(s_misc, misc_before(b, j, "tail"))
                        for h in range(2):
                            last = pe.matmul(misc[:, NQ * h:NQ * h + NQ], dtwT[:, P * h:P * h + P], dlo[:], start=True, stop=True)
                        last.then_inc(s_t5, 1)
                    if batch_live(b, 3) and j == 1:
                        pe.wait_ge(s_misc, misc_before(b, j, "y"))
                        pe.wait_ge(s_y, b - 2)
                        for h in range(2):
                            last = pe.matmul(misc[half(nxt), 0:DM], yT[:, h, :], opT[:, h, :], start=h == 0, stop=h == 1)
                        last.then_inc(s_t6, 1)
                    if tile_live(b, j, 1):
                        pv_group(t - 1, 2, pv_rows)
                        pv_group(t - 1, 3, pv_rows)

            pipeline(pe, body)

            pe.wait_ge(s_fq, 1)
            xd = flat(dA[0]).rearrange("p (r d) -> p r d", r=RT)
            for r in range(RT):
                wait(pe, s_fa, 2 + r - 1)
                for h in range(2):
                    last = pe.transpose(bank[r % 2][:, P * h:P * h + P], xd[:, r, P * h:P * h + P], ident[:])
                last.then_inc(s_fpe, 1)
                pe.wait_ge(s_fa, 2 + r + 1)
                wait(pe, s_fev, r - 1)
                for h in range(2):
                    last = pe.matmul(bank[2 + r % 2][:, 0:DM], xdT[:, r, P * h:P * h + P], wdT[:, h, :],
                                     start=h == 0, stop=h == 1)
                last.then_inc(s_fpe, 1)


_INS = ['x', 'ctx_768', 'L0_xattn_Wq', 'L0_xattn_Wk', 'L0_xattn_Wv', 'L0_xattn_Wo', 'L0_xattn_bo',
        'L0_attn_norm_w', 'L0_attn_x_proj_w', 'L0_attn_dt_proj_w', 'L0_attn_dt_proj_b', 'L0_attn_A_log',
        'L0_attn_D', 'L0_attn_out_proj_w', 'L0_ffn_weight', 'L0_ffn_bias']


def kernel(**inputs):
    import numpy as _np
    import concourse.bacc as _bacc
    from concourse import mybir as _mybir
    from concourse.bass_utils import run_bass_kernel_spmd as _run

    nc = _bacc.Bacc("TRN2", target_bir_lowering=False, num_devices=1)
    arrays, args = {}, []
    for name in _INS:
        a = _np.ascontiguousarray(inputs[name])
        arrays[f"in_{name}"] = a
        args.append(nc.dram_tensor(f"in_{name}", a.shape, _mybir.dt.from_np(a.dtype), kind="ExternalInput").ap())
    shape = inputs['x'].shape
    o = nc.dram_tensor("out_0", shape, _mybir.dt.float32, kind="ExternalOutput").ap()
    perceiver_layer(nc, *args, o)
    r = _run(nc, [arrays], core_ids=[0])
    return r.results[0]["out_0"]
```

```python
from contextlib import ExitStack

import concourse.bass as bass
from concourse import mybir

F32 = mybir.dt.float32
F32R = mybir.dt.float32r
ALU = mybir.AluOpType
ACT = mybir.ActivationFunctionType
AX = mybir.AxisListType

P = 128
LN_EPS = 1e-5
RMS_EPS = 1e-6
FP6_MAX = 7.5
FP6_BLOCK = 32
SCALE_FLOOR = 1e-30
ROUND = 1.5 * 2.0 ** 23

FIRST, LOOP_FROM, LOOP_TO, LAST = -1, 3, 7, 10


def perceiver_layer(nc, x, ctx, Wq, Wk, Wv, Wo, bo, norm_w, x_proj_w, dt_proj_w, dt_proj_b,
                    A_log, D, out_proj_w, ffn_w, ffn_b, out):
    NB, NQ, DM = x.shape
    NK, DC = ctx.shape[1], ctx.shape[2]
    INNER = Wq.shape[1]
    DH = 64
    TILES = INNER // P
    NT = NB * TILES
    DT = DC - P
    KT = -(-NK // P)
    KLAST = NK - (KT - 1) * P
    NKP = NK + NK % 2
    NG = -(-KT // 4)
    GROUPS = [(-(-KT * g // NG), -(-KT * (g + 1) // NG) - -(-KT * g // NG)) for g in range(NG)]
    CHUNKS = [(k * P, min(n * P, NK - k * P)) for k, n in GROUPS]
    RH, RW = DC + 2, 2 * DC + 2
    STATE = A_log.shape[1]
    RANK = dt_proj_w.shape[1]
    NS = 16
    SLICES = 2 * STATE // NS
    SG = STATE // NS
    RT = NB * NQ // P
    assert NG == len(CHUNKS) == SG == 4 and TILES == SLICES == NB == 8 and NQ == DH and DM == 2 * P

    es = ExitStack()
    with es:
        def sb(name, shape, dt=F32):
            return es.enter_context(nc.sbuf_tensor(name, shape, dt))

        def sem(name):
            return es.enter_context(nc.semaphore(name))

        ident = sb("ident", [P, P])
        wkT = sb("wkT", [P, TILES, 2 * P])
        wv_a = sb("wv_a", [P, INNER])
        wv_b = sb("wv_b", [DT, INNER])
        wo = sb("wo", [P, TILES, DM])
        xpT = sb("xpT", [P, 2, RANK + 2 * STATE])
        dtwT = sb("dtwT", [RANK, DM])
        opT = sb("opT", [P, 2, DM])
        wdT = sb("wdT", [P, 2, DM])
        negA = sb("negA", [P, 2, STATE])
        cols = sb("cols", [P, 3, 2])
        norm_c, dtb_c, D_c = cols[:, 0, :], cols[:, 1, :], cols[:, 2, :]
        one_c = sb("one_c", [P, 1])
        bias_r = sb("bias_r", [P, DM])
        x_rows = sb("x_rows", [P, RT, DM])

        raw = [sb(f"raw{i}", [P, 4, P + 2 * DT]) for i in range(2)]
        rows = [sb(f"rows{i}", [P, KT, RW], F32R) for i in range(2)]
        ctH = [sb(f"ctH{i}", [P, NKP], F32R) for i in range(2)]
        ctL = [sb(f"ctL{i}", [P, NKP], F32R) for i in range(2)]
        ctT = [sb(f"ctT{i}", [P, NKP], F32R) for i in range(2)]
        qd = [sb(f"qd{i}", [P, TILES, P]) for i in range(2)]
        qpH = [sb(f"qpH{i}", [P, 2, P], F32R) for i in range(2)]
        qpL = [sb(f"qpL{i}", [P, 2, P], F32R) for i in range(2)]
        cmax = sb("cmax", [P, NG])
        nmax = sb("nmax", [P, 2])
        prob = sb("prob", [P, NK])
        ptH = [sb(f"ptH{i}", [P, 4, P], F32R) for i in range(2)]
        ptL = [sb(f"ptL{i}", [P, 4, P], F32R) for i in range(2)]
        rinv = sb("rinv", [P, 1])
        olow = sb("olow", [P, DC])
        osb = [sb(f"osb{i}", [P, DC]) for i in range(2)]
        oT = sb("oT", [P, 2, P])
        ao = [sb(f"ao{i}", [P, TILES, NQ]) for i in range(2)]

        st = sb("st", [P, RT, 6])
        mv = sb("mv", [P, RT, 2])
        ve = sb("ve", [P, RT])
        rs0 = sb("rs0", [P, RT])
        rs1 = sb("rs1", [P, RT])
        xln = sb("xln", [P, 2, DM])
        xnT = sb("xnT", [P, 2, NQ])
        bc = sb("bc", [P, NQ])
        dlo = sb("dlo", [RANK, NQ])
        zdt = sb("zdt", [P, 2, NQ])
        sp1 = sb("sp1", [P, 2, NQ])
        dt_ = [sb(f"dt{i}", [P, 2, NQ]) for i in range(2)]
        dtx = [sb(f"dtx{i}", [P, 2, NQ]) for i in range(2)]
        ypart = [sb(f"ypart{i}", [P, 2, SG + 1, NQ]) for i in range(2)]
        yT = sb("yT", [P, 2, NQ])
        fq = [sb(f"fq{i}", [P, DM]) for i in range(2)]
        fqT = sb("fqT", [P, 2, NQ])
        fscale = sb("fscale", [P, 2, DM // FP6_BLOCK])
        bcr = [sb(f"bcr{i}", [P, 2, NS * NQ]) for i in range(2)]
        dA = [sb(f"dA{i}", [P, NS, NQ]) for i in range(2)]
        hs = [sb(f"hs{i}", [P, NS, NQ]) for i in range(2)]

        bank = [es.enter_context(nc.psum_tensor(f"bank{i}", [P, 512], F32)) for i in range(8)]
        pt_bank = [bank[4], bank[5]]
        o_bank = bank[6]
        misc = bank[7]
        ao_bank = bank[NG - 1]
        bc_scratch = nc.dram_tensor("bc_scratch", [NB, P, NQ], F32, kind="Internal").ap()
        q_scratch = nc.dram_tensor("q_scratch", [NB, P, TILES, NQ], F32, kind="Internal").ap()

        def flat(t):
            return t[:] if len(t.shape) == 2 else t[:].rearrange("p a b -> p (a b)")

        wq_v = [flat(dA[0]), flat(dA[1])]
        wk_a, wk_b = flat(hs[0]), flat(hs[1])[0:DT, :]
        x0 = bcr[0][:, 0, :].rearrange("p (r d) -> p r d", r=RT)
        xT0 = bcr[0][:, 1, :].rearrange("p (h n) -> p h n", h=2)
        op_rows = bcr[1][:, 0, 0:2 * DM].rearrange("p (h d) -> p h d", h=2)
        fw_rows = bcr[1][:, 0, 2 * DM:4 * DM].rearrange("p (h d) -> p h d", h=2)
        q_stage = [bcr[1][:, 1, 512 * i:512 * i + 512] for i in range(2)]
        yp0, yp1 = [y[:].rearrange("p a b c -> p (a b c)") for y in ypart]
        xp_bc, xp_dt = yp0[:, 0:DM], yp0[0:RANK, DM:2 * DM]
        dtw_rows = yp1[:, 0:2 * RANK].rearrange("p (h r) -> p h r", h=2)
        bo_r = yp1[:, DM:2 * DM]

        s_wq, s_wk, s_w, s_x = sem("wq_loaded"), sem("wk_loaded"), sem("weights_loaded"), sem("x_loaded")
        s_raw = [sem("raw_loaded0"), sem("raw_loaded1")]
        s_id0, s_ident = sem("ident_cleared"), sem("ident_ready")
        s_ope = [sem("open_psum_act"), sem("open_psum_dve")]
        s_oev = [sem("open_copied_act"), sem("open_copied_dve")]
        s_odve, s_oact = sem("open_dve"), sem("open_act")
        s_qst = [sem("q_stored0"), sem("q_stored1")]
        s_opened = sem("opened")
        s_qd = [sem("queries_placed0"), sem("queries_placed1")]
        s_qp, s_qpH = sem("qprime_summed"), sem("qprime_high")
        s_scores, s_cmax, s_nmax, s_exp = sem("scores_summed"), sem("chunk_max"), sem("negmax"), sem("exp_done")
        s_pt, s_ptH, s_ptL = sem("prob_transposed"), sem("prob_high"), sem("prob_low")
        s_pv, s_och, s_o = sem("pv_summed"), sem("o_chain"), sem("o_normalized")
        s_oT, s_ao, s_aoc = sem("o_transposed"), sem("ao_summed"), sem("ao_copied")
        s_ct, s_ctH = sem("ctx_transposed"), sem("ctx_high")
        s_rowH, s_rowL = sem("rows_high"), sem("rows_low")
        s_misc = sem("misc_bank_free")
        s_t1, s_t2, s_t4, s_t5, s_t6 = (sem(n) for n in ("out_projected", "norms_transposed", "bc_projected",
                                                        "dt_projected", "y_projected"))
        s_var, s_rsq, s_norm = sem("variances"), sem("rsqrt_guess"), sem("x_normalized")
        s_tch, s_ach = sem("tail_dve_chain"), sem("tail_act_chain")
        s_bcst, s_sp, s_dt = sem("bc_stored"), sem("softplus_log"), sem("dt_ready")
        s_bcr = [sem("bc_group_loaded0"), sem("bc_group_loaded1")]
        s_dta, s_u, s_dA = sem("dta_ready"), sem("u_ready"), sem("decay_ready")
        s_scan, s_hc, s_red, s_y = sem("scan_done"), sem("hc_ready"), sem("slice_reduced"), sem("y_ready")
        s_fch, s_fvar, s_fln, s_frsq = (sem(n) for n in ("ffn_dve_chain", "ffn_variance", "ffn_log", "ffn_rsqrt_guess"))
        s_fq, s_fT, s_fmm = sem("ffn_quantized"), sem("ffn_transposed"), sem("ffn_projected")
        s_fwq, s_fwT = sem("ffn_weight_quantized"), sem("ffn_weight_transposed")
        s_out = sem("out_stored")
        s_settled = sem("settled")
        s_dzero, s_dst, s_ws = sem("decay_zeroed"), sem("open_stats"), sem("small_weights_loaded")
        s_cleared = sem("constants_cleared")

        def tile_live(b, j, lag):
            return not isinstance(b, int) or 0 <= TILES * b + j - lag < NT

        def batch_live(b, lag):
            return not isinstance(b, int) or 0 <= b - lag < NB

        def misc_uses(b, j):
            return ([("q", tile_live(b, j, -1)), ("oT", tile_live(b, j, 3)), ("ctx", batch_live(b, -1)),
                     ("tail", batch_live(b, 1) and j in (2, 4, 5, 6)),
                     ("y", batch_live(b, 3) and j == 1), ("fw", isinstance(b, int) and b == 0 and j == 7),
                     ("fT", batch_live(b, 3) and j == 7), ("fmm", batch_live(b, 3) and j == 7)])

        def misc_in(b):
            return sum(bool(live) for j in range(TILES) for _, live in misc_uses(b, j))

        def misc_before(b, j, kind):
            n = 0
            if isinstance(b, int):
                n = sum(misc_in(i) for i in range(FIRST, b))
            else:
                n = (b - LOOP_FROM) * misc_in(LOOP_FROM) + sum(misc_in(i) for i in range(FIRST, LOOP_FROM))
            n += sum(bool(live) for i in range(j) for _, live in misc_uses(b, i))
            for k, live in misc_uses(b, j):
                if k == kind:
                    return n
                n += bool(live)

        def pipeline(eng, body):
            for b in range(FIRST, LOOP_FROM):
                body(b, b % 2)
            with eng.Fori(0, (LOOP_TO - LOOP_FROM) // 2) as i:
                body(2 * i + LOOP_FROM, LOOP_FROM % 2)
                body(2 * i + LOOP_FROM + 1, 1 - LOOP_FROM % 2)
            for b in range(LOOP_TO, LAST + 1):
                body(b, b % 2)

        def late(batch, s):
            return isinstance(batch, int) and SLICES * batch + s >= SLICES * (NB - 2) + 2

        def raw_loaded(batch, g):
            if g % 2 == 0:
                return 64 * batch + 32 * (g // 2 + 1)
            return 96 * batch + (32 if g == 1 else 96)

        def key_rows(kt):
            return P if kt < KT - 1 else KLAST

        def wait(eng, s, value):
            if not isinstance(value, int) or value > 0:
                eng.wait_ge(s, value)

        def settle(eng):
            eng.sem_inc(s_settled, 1)

        def half(par):
            return slice(NQ * par, NQ * par + NQ)

        def residual(b, par):
            v = x_rows[half(par)].rearrange("p r (c d) -> p (r c) d", c=2)
            if isinstance(b, int):
                return x_rows[half(par), b // 2, :]
            return v[:, bass.ds(b - par, 2), :].rearrange("p c d -> p (c d)")

        O_LN0 = 1 + 4 + 1
        TAIL_STEPS = 7
        FFN_STEPS = 24

        OPEN_ACT, OPEN_DVE = 0, 1
        OPEN_BY = [k % 2 for k in range(8 + 2 + 8 + 3)]
        OPEN_BANKS = [[bank[0], bank[1]], [bank[2], bank[3]]]
        O_WK, O_X, O_Q, O_XP, O_DTW, O_OP = 0, 8, 10, 18, 19, 20

        def open_place(k):
            who = OPEN_BY[k]
            n = sum(w == who for w in OPEN_BY[:k])
            return who, n, OPEN_BANKS[who][n % 2]

        block = es.enter_context(nc.Block())

        @block.sync
        def _(sp):
            sp.dma_start(x_rows[:], x.rearrange("(r a) q d -> (a q) r d", a=2)).then_inc(s_x, 16)
            sp.dma_start(wk_a, Wk[0:P, :]).then_inc(s_wk, 16)
            sp.dma_start(wk_b, Wk[P:DC, :]).then_inc(s_wk, 16)

            def load_raw(batch, g):
                k0, n = GROUPS[g]
                parts = [(0, n, P)] if k0 + n < KT else [(0, n - 1, P), (n - 1, n, KLAST)]
                for k, k_end, rest in parts:
                    keys = slice((k0 + k) * P, (k0 + k_end - 1) * P + rest)
                    dst = raw[g % 2][0:rest, k:k_end, :]
                    if isinstance(batch, int):
                        src = ctx[batch, keys, :]
                    else:
                        src = ctx[bass.ds(batch, 1), keys, :].rearrange("o k d -> (o k) d")
                    src = src.rearrange("(n p) d -> p n d", n=k_end - k)
                    sp.dma_start(dst[:, :, 0:DC], src).then_inc(s_raw[g % 2], 16)
                    sp.dma_start(dst[:, :, DC:], src[:, :, P:DC]).then_inc(s_raw[g % 2], 16)

            load_raw(0, 0)
            sp.dma_start(wq_v[0], Wq[0:P, :]).then_inc(s_wq, 16)
            sp.dma_start(wq_v[1], Wq[P:2 * P, :]).then_inc(s_wq, 16)
            load_raw(0, 1)
            for dst, src in (
                (xp_bc, x_proj_w[RANK:RANK + 2 * STATE, :]), (xp_dt, x_proj_w[0:RANK, :]),
                (dtw_rows, dt_proj_w.rearrange("(h p) r -> p h r", h=2)),
                (op_rows, out_proj_w.rearrange("(h p) d -> p h d", h=2)),
                (fw_rows, ffn_w.rearrange("(h p) d -> p h d", h=2)),
                (negA[:], A_log.rearrange("(h p) n -> p h n", h=2)), (bo_r, bo.partition_broadcast(P)),
            ):
                sp.dma_start(dst, src).then_inc(s_ws, 16)
            for dst, src in (
                (wv_a[:], Wv[0:P, :]), (wv_b[:], Wv[P:DC, :]),
                (wo[:], Wo.rearrange("(t p) d -> p t d", p=P)), (bias_r[:], ffn_b.partition_broadcast(P)),
            ):
                sp.dma_start(dst, src).then_inc(s_w, 16)
            with nc.allow_non_contiguous_dma(reason="256 values each, once"):
                for dst, src in ((norm_c, norm_w), (dtb_c, dt_proj_b), (D_c, D)):
                    sp.dma_start(dst, src.rearrange("(h p) -> p h", h=2)).then_inc(s_w, 16)

            def opening(j):
                for m in {2: (0, 1), 3: (2, 3), 4: (4, 5), 5: (6, 7)}.get(j, ()):
                    who, n, _ = open_place(O_Q + m)
                    sp.wait_ge(s_oev[who], n + 1)
                    sp.dma_start(q_scratch[:, :, m, :].rearrange("b p q -> p b q"),
                                 q_stage[m % 2].rearrange("p (b q) -> p b q", b=NB)).then_inc(s_qst[m % 2], 16)
                if j == 7:
                    for i in range(2):
                        sp.wait_ge(s_qst[i], 16 * TILES // 2)
                    sp.wait_ge(s_cleared, 1)
                    sp.sem_inc(s_opened, 1)

            def load_bc(batch, g):
                if isinstance(batch, int):
                    src = bc_scratch[batch]
                else:
                    src = bc_scratch[bass.ds(batch, 1)].rearrange("o s q -> (o s) q")
                src = src.rearrange("(w g n) q -> w g (n q)", w=2, g=SG)[:, g, :]
                sp.dma_start(bcr[g % 2][:], src.partition_broadcast(P)).then_inc(s_bcr[g % 2], 16)

            def load_queries(b, par):
                nxt = 1 - par
                wait(sp, s_qp, TILES * b)
                settle(sp)
                for h in range(2):
                    if isinstance(b, int):
                        src = q_scratch[b + 1, half(h)]
                    else:
                        src = q_scratch[bass.ds(b + 1, 1), half(h)].rearrange("o p t q -> (o p) t q")
                    sp.dma_start(qd[nxt][half(h), :, half(h)], src).then_inc(s_qd[nxt], 16)

            def body(b, par):
                first = isinstance(b, int) and b == FIRST
                if isinstance(b, int) and b == 0:
                    sp.wait_ge(s_opened, 5)
                if batch_live(b, -1) and not first:
                    load_queries(b, par)
                for j in range(TILES):
                    if first:
                        opening(j)
                        if j == 7:
                            load_queries(b, par)
                    if batch_live(b, 2) and j == 0:
                        wait(sp, s_hc, SLICES * (b - 2))
                        settle(sp)
                        load_bc(b - 2, 1)
                    if batch_live(b, 2) and j in (2, 4):
                        sp.wait_ge(s_hc, SLICES * (b - 2) + j)
                        settle(sp)
                        load_bc(b - 2, j // 2 + 1)
                    if j % 2 == 1:
                        g = j // 2
                        nb, ng = (b + 1, g + 2) if g < 2 else (b + 2, g - 2)
                        if batch_live(b, -1):
                            sp.wait_ge(s_ct, 8 * (b + 1) + j + 1)
                            settle(sp)
                            sp.wait_ge(s_rowH, NG * (b + 1) + g + 1)
                            settle(sp)
                            sp.wait_ge(s_rowL, NG * (b + 1) + g + 1)
                            settle(sp)
                            if not isinstance(nb, int):
                                load_raw(nb % NB, ng)
                            elif nb < NB:
                                load_raw(nb, ng)
                    if batch_live(b, 1) and j == 6:
                        sp.wait_ge(s_misc, misc_before(b, 5, "tail") + 1)
                        settle(sp)
                        if isinstance(b, int):
                            dst = bc_scratch[b - 1]
                        else:
                            dst = bc_scratch[bass.ds(b - 1, 1)].rearrange("o s q -> (o s) q")
                        sp.dma_start(dst, bc[:]).then_inc(s_bcst, 16)
                    if batch_live(b, 1) and j == 7:
                        sp.wait_ge(s_bcst, 16 * b)
                        settle(sp)
                        wait(sp, s_hc, SLICES * (b - 1) - 2)
                        settle(sp)
                        load_bc(b - 1, 0)
                    if batch_live(b, 3) and j == 7:
                        sp.wait_ge(s_misc, misc_before(b, j, "fmm") + 1)
                        settle(sp)
                        if isinstance(b, int):
                            dst = out[b - 3]
                        else:
                            dst = out[bass.ds(b - 3, 1)].rearrange("o q d -> (o q) d")
                        sp.dma_start(dst, residual(b - 3, 1 - par)).then_inc(s_out, 16)

            pipeline(sp, body)
            sp.wait_ge(s_out, 16 * NB)

        @block.gpsimd
        def _(pool):
            pool.memset(ident[:], 0.0).then_inc(s_id0, 1)
            pool.wait_ge(s_id0, 1)
            pool.affine_select(out=ident[:], in_=ident[:], compare_op=ALU.not_equal, fill=1.0, base=0,
                               pattern=[[-1, P]], channel_multiplier=1).then_inc(s_ident, 1)
            pool.memset(one_c[:], 1.0)
            for i in range(2):
                pool.memset(qd[i][:], 0.0)
                pool.memset(rows[i][:, :, DC:DC + 1].bitcast(F32), 1.0)
                pool.memset(rows[i][:, :, DC + 1:RH].bitcast(F32), 0.0)
                pool.memset(ctH[i][:, NK:NKP].bitcast(F32), 0.0)
                pool.memset(ctL[i][:, NK:NKP].bitcast(F32), 0.0)
                pool.memset(ctT[i][:, NK:NKP].bitcast(F32), 0.0)
            pool.memset(zdt[:], 0.0).then_inc(s_cleared, 1)
            pool.wait_ge(s_cleared, 1)
            pool.sem_inc(s_opened, 1)

            def hc(batch, s):
                k = SLICES * batch + s
                g = s // 2
                pool.wait_ge(s_scan, k + 1)
                pool.tensor_tensor(hs[s % 2][:], hs[s % 2][:],
                                   bcr[g % 2][:, 1, :].rearrange("p (n q) -> p n q", n=NS), ALU.mult).then_inc(s_hc, 1)

            def prepare(batch, par, s):
                k = SLICES * batch + s
                g, h = s // 2, s % 2
                wait(pool, s_scan, k - 1)
                if not late(batch, s):
                    pool.tensor_tensor(dA[s % 2][:, :, 1:NQ],
                                   dt_[par][:, h, 1:NQ].unsqueeze(1).broadcast_to([P, NS, NQ - 1]),
                                   negA[:, h, NS * g:NS * g + NS].unsqueeze(2).broadcast_to([P, NS, NQ - 1]),
                                   ALU.mult).then_inc(s_dta, 1)
                wait(pool, s_red, k - 1)
                pool.wait_ge(s_bcr[g % 2], 16 * (2 * batch + g // 2 + 1))
                pool.tensor_tensor(hs[s % 2][:],
                                   dtx[par][:, h, :].unsqueeze(1).broadcast_to([P, NS, NQ]),
                                   bcr[g % 2][:, 0, :].rearrange("p (n q) -> p n q", n=NS), ALU.mult).then_inc(s_u, 1)

            def body(b, par):
                if isinstance(b, int) and b == 1:
                    pool.wait_ge(s_opened, 5)
                    pool.wait_ge(s_fwq, 1)
                    for i in range(2):
                        last = pool.memset(dA[i][:, :, 0:1], 0.0)
                    last.then_inc(s_dzero, 1)
                for j in range(TILES):
                    if batch_live(b, 3) and j == 0 and not late(b - 3, SLICES - 1):
                        hc(b - 3, SLICES - 1)
                    if batch_live(b, 2):
                        if j == 0:
                            pool.wait_ge(s_dt, b - 1)
                            prepare(b - 2, par, 0)
                        elif not late(b - 2, j - 1):
                            hc(b - 2, j - 1)
                        if j + 1 < SLICES:
                            prepare(b - 2, par, j + 1)
                    if batch_live(b, -1) and j % 2 == 1:
                        g = j // 2
                        k0, n = GROUPS[g]
                        nxt = 1 - par
                        pool.wait_ge(s_rowH, NG * (b + 1) + g + 1)
                        pool.tensor_tensor(rows[nxt][:, k0:k0 + n, RH:RW], raw[g % 2][:, 0:n, 0:DC],
                                           rows[nxt][:, k0:k0 + n, 0:DC].bitcast(F32),
                                           ALU.subtract).then_inc(s_rowL, 1)

            pipeline(pool, body)

        @block.scalar
        def _(act):
            step = [0]

            def link(ins, s=s_oact):
                step[0] += 1
                ins.then_inc(s, 1)
                act.wait_ge(s, step[0])

            def open_copy(k, dst, shape=None, scale=1.0):
                who, n, bk = open_place(k)
                act.wait_ge(s_ope[who], n + 1)
                act.activation(dst, shape(bk), ACT.Copy, scale=scale).then_inc(s_oev[who], 1)

            nc.scalar.preload_act_table_set("natural_log_exp_and_others")
            act.wait_ge(s_odve, 1)
            link(act.activation(rs0[:], ve[:], ACT.Ln))
            link(act.activation(rs1[:], rs0[:], ACT.Exp, scale=-0.5))

            def opening(j):
                if j == 1:
                    for m in range(0, TILES, 2):
                        open_copy(O_WK + m, wkT[:, m, :], lambda bk: bk[:, 0:2 * P])
                    open_copy(O_X, xT0[:, 0, :], lambda bk: bk[:])
                if j in (2, 3, 4, 5):
                    m = 2 * (j - 2)
                    if m >= 2:
                        act.wait_ge(s_qst[m % 2], 16 * (m // 2))
                    open_copy(O_Q + m, q_stage[m % 2], lambda bk: bk[:], scale=DH ** -0.5)
                if j == 6:
                    open_copy(O_XP, xpT[:], lambda bk: bk[:, 0:2 * (RANK + 2 * STATE)].rearrange("p (h n) -> p h n", h=2))
                    open_copy(O_OP, opT[:], lambda bk: bk[:].rearrange("p (h n) -> p h n", h=2))
                    act.wait_ge(s_ws, 16 * 7)
                    link(act.activation(negA[:], negA[:], ACT.Exp))
                if j == 7:
                    act.wait_ge(s_oev[OPEN_ACT], sum(w == OPEN_ACT for w in OPEN_BY))
                    act.sem_inc(s_opened, 1)

            def high_of_group(t, g):
                k0, n = GROUPS[g]
                act.wait_ge(s_pt, NG * t + g + 1)
                wait(act, s_pv, NG * t + g - 1)
                act.activation(ptH[g % 2][:, 0:n, :], pt_bank[g % 2][:, 0:n * P].rearrange("p (n q) -> p n q", n=n),
                               ACT.Copy).then_inc(s_ptH, 1)

            def exp_of_chunk(t, c):
                c0, n = CHUNKS[c]
                act.wait_ge(s_nmax, t + 1)
                wait(act, s_pt, NG * (t - 1) + c + 1)
                act.activation(prob[:, c0:c0 + n], bank[c][:, 0:n], ACT.Exp, bias=nmax[:, 0:1]).then_inc(s_exp, 1)

            def decay(b, par, s):
                k = SLICES * (b - 2) + s
                if late(b - 2, s):
                    act.wait_ge(s_dt, b - 1)
                    act.wait_ge(s_scan, k - 1)
                    for n in range(NS):
                        last = act.activation(dA[s % 2][:, n, 1:NQ], dt_[par][:, s % 2, 1:NQ], ACT.Exp,
                                              scale=negA[:, s % 2, NS * (s // 2) + n:NS * (s // 2) + n + 1])
                    last.then_inc(s_dA, 1)
                else:
                    act.wait_ge(s_dta, k + 1)
                    act.activation(dA[s % 2][:, :, 1:NQ], dA[s % 2][:, :, 1:NQ], ACT.Exp).then_inc(s_dA, 1)

            def body(b, par):
                nxt = 1 - par
                B = b - 1
                if isinstance(b, int) and b == 0:
                    act.wait_ge(s_opened, 5)
                for j in range(TILES):
                    t = TILES * b + j
                    if isinstance(b, int) and b == FIRST:
                        opening(j)
                    if tile_live(b, j, -1):
                        i = (j + 1) % 2
                        act.wait_ge(s_qp, t + 2)
                        act.activation(qpH[i][:].rearrange("p a q -> p (a q)"), misc[:, 0:2 * P], ACT.Copy).then_inc(s_qpH, 1)
                    if batch_live(b, 3) and j == 2:
                        h = half(nxt)
                        act.wait_ge(s_fvar, b - 2)
                        act.activation(rs0[h, 2:3], ve[h, 2:3], ACT.Ln).then_inc(s_fln, 1)
                        act.wait_ge(s_fln, b - 2)
                        act.activation(rs1[h, 2:3], rs0[h, 2:3], ACT.Exp, scale=-0.5).then_inc(s_frsq, 1)
                    if tile_live(b, j, 1):
                        exp_of_chunk(t - 1, 1)
                        exp_of_chunk(t - 1, 2)
                        high_of_group(t - 1, 0)
                    if tile_live(b, j, 3):
                        act.wait_ge(s_oT, t - 2)
                        act.activation(oT[:, 0, :], misc[:, 0:P], ACT.Copy)
                        act.activation(oT[0:DT, 1, :], misc[0:DT, P:2 * P], ACT.Copy).then_inc(s_misc, 1)
                    if tile_live(b, j, 1):
                        exp_of_chunk(t - 1, 3)
                        high_of_group(t - 1, 1)
                    if batch_live(b, -1):
                        g = j // 2
                        k0, n = GROUPS[g]
                        w = min(n * P, NK - k0 * P)
                        dst = (ctH, ctT)[j % 2][nxt]
                        act.wait_ge(s_ct, 8 * (b + 1) + j + 1)
                        act.activation(dst[:, k0 * P:k0 * P + w], misc[:, 0:w], ACT.Copy).then_inc(s_ctH, 1)
                    if batch_live(b, 2) and j == 0:
                        decay(b, par, 0)
                    if batch_live(b, 1) and j == 3:
                        act.wait_ge(s_var, b)
                        act.activation(rs0[half(nxt), 0:2], ve[half(nxt), 0:2], ACT.Ln).then_inc(s_ach, 1)
                        act.wait_ge(s_ach, 2 * B + 1)
                        act.activation(rs1[half(nxt), 0:2], rs0[half(nxt), 0:2], ACT.Exp, scale=-0.5).then_inc(s_rsq, 1)
                    if batch_live(b, -1) and j % 2 == 1:
                        g = j // 2
                        k0, n = GROUPS[g]
                        act.wait_ge(s_raw[g % 2], raw_loaded(b + 1, g))
                        wait(act, s_pv, NG * TILES * b)
                        act.activation(rows[nxt][:, k0:k0 + n, 0:DC], raw[g % 2][:, 0:n, 0:DC], ACT.Copy).then_inc(s_rowH, 1)
                    if tile_live(b, j, 1):
                        high_of_group(t - 1, 2)
                    if tile_live(b, j, 3):
                        act.wait_ge(s_ao, t - 2)
                        tl = (j - 3) % TILES
                        act.activation(ao[par if j >= 3 else nxt][:, tl, :], ao_bank[:, 0:NQ], ACT.Copy).then_inc(s_aoc, 1)
                    if tile_live(b, j, 1):
                        high_of_group(t - 1, 3)
                    if batch_live(b, 3) and j == 7:
                        act.wait_ge(s_fT, b - 2)
                        act.activation(fqT[:].rearrange("p h q -> p (h q)"), misc[:, 0:2 * NQ], ACT.Copy).then_inc(s_misc, 1)
                    if isinstance(b, int) and b == 0 and j == 7:
                        act.wait_ge(s_fwT, 1)
                        act.activation(wdT[:].rearrange("p h q -> p (h q)"), misc[:], ACT.Copy).then_inc(s_misc, 1)
                    if batch_live(b, 1) and j == 4:
                        act.wait_ge(s_t2, b)
                        for h in range(2):
                            act.activation(ypart[nxt][:, h, SG, :], misc[:, NQ * h:NQ * h + NQ], ACT.Copy, scale=D_c[:, h:h + 1])
                            last = act.activation(xnT[:, h, :], misc[:, NQ * (2 + h):NQ * (3 + h)], ACT.Copy,
                                                  scale=norm_c[:, h:h + 1])
                        last.then_inc(s_misc, 1)
                    if batch_live(b, 1) and j == 5:
                        act.wait_ge(s_t4, b)
                        wait(act, s_bcst, 16 * B)
                        act.activation(bc[:], misc[:, 0:NQ], ACT.Copy)
                        act.activation(dlo[:], misc[0:RANK, NQ:2 * NQ], ACT.Copy).then_inc(s_misc, 1)
                    if batch_live(b, 1) and j == 6:
                        act.wait_ge(s_t5, b)
                        wait(act, s_dt, B)
                        for h in range(2):
                            last = act.activation(zdt[:, h, :], misc[:, NQ * h:NQ * h + NQ], ACT.Identity,
                                                  bias=dtb_c[:, h:h + 1])
                        last.then_inc(s_misc, 1)
                    if tile_live(b, j, 0):
                        exp_of_chunk(t, 0)
                    if batch_live(b, 2) and j + 1 < SLICES:
                        decay(b, par, j + 1)
                    if batch_live(b, 1) and j == 6:
                        act.wait_ge(s_misc, misc_before(b, j, "tail") + 1)
                        act.activation(sp1[:], zdt[:], ACT.Abs).then_inc(s_ach, 1)
                        act.wait_ge(s_ach, 2 * b)
                        act.activation(sp1[:], sp1[:], ACT.Exp, scale=-1.0).then_inc(s_sp, 1)
                        act.wait_ge(s_sp, 2 * B + 1)
                        act.activation(sp1[:], sp1[:], ACT.Ln, bias=one_c[:]).then_inc(s_sp, 1)

            pipeline(act, body)

        @block.vector
        def _(dve):
            step = [0]

            def link(ins):
                step[0] += 1
                ins.then_inc(s_odve, 1)
                dve.wait_ge(s_odve, step[0])

            def open_copy(k, dst, shape, scale=None):
                who, n, bk = open_place(k)
                dve.wait_ge(s_ope[who], n + 1)
                if scale is None:
                    dve.tensor_copy(dst, shape(bk)).then_inc(s_oev[who], 1)
                else:
                    dve.tensor_scalar(dst, shape(bk), scale, None, ALU.mult).then_inc(s_oev[who], 1)

            def newton(link, r1, r0, v):
                link(0, dve.tensor_tensor(r0, r1, r1, ALU.mult))
                link(1, dve.tensor_tensor(r0, r0, v, ALU.mult))
                link(2, dve.tensor_scalar(r0, r0, -0.5, 1.5, ALU.mult, ALU.add))
                link(3, dve.tensor_tensor(r0, r0, r1, ALU.mult))

            def mx_quantize(v, a, b, c, d, scale, inv):
                vb, ab, db = (m.rearrange("p (k e) -> p k e", e=FP6_BLOCK) for m in (v, a, d))
                shape = list(vb.shape)
                return [
                    lambda: dve.tensor_reduce(scale, vb, AX.X, ALU.max, apply_absolute_value=True),
                    lambda: dve.tensor_scalar(scale, scale, 1.0 / FP6_MAX, SCALE_FLOOR, ALU.mult, ALU.max),
                    lambda: dve.reciprocal(inv, scale),
                    lambda: dve.tensor_tensor(ab, vb, inv.unsqueeze(2).broadcast_to(shape), ALU.mult),
                    lambda: dve.tensor_tensor(b, a, a, ALU.mult),
                    lambda: dve.tensor_scalar(c, b, 16.0, None, ALU.is_ge),
                    lambda: dve.tensor_scalar(b, b, 4.0, None, ALU.is_ge),
                    lambda: dve.tensor_scalar(d, c, -2.0, 8.0, ALU.mult, ALU.add),
                    lambda: dve.scalar_tensor_tensor(d, b, -4.0, d, ALU.mult, ALU.add),
                    lambda: dve.tensor_tensor(a, a, d, ALU.mult),
                    lambda: dve.tensor_scalar(b, b, -0.125, -0.125, ALU.mult, ALU.add),
                    lambda: dve.scalar_tensor_tensor(b, c, 1.0, b, ALU.add, ALU.mult),
                    lambda: dve.tensor_scalar(d, a, ROUND, ROUND, ALU.add, ALU.subtract),
                    lambda: dve.tensor_tensor(a, d, a, ALU.subtract),
                    lambda: dve.scalar_tensor_tensor(d, a, 0.5, d, ALU.is_ge, ALU.subtract),
                    lambda: dve.tensor_tensor(d, d, b, ALU.mult),
                    lambda: dve.tensor_tensor(ab, db, scale.unsqueeze(2).broadcast_to(shape), ALU.mult),
                ]

            dve.wait_ge(s_x, 16)
            for r in range(RT):
                last = dve.bn_stats(st[:, r, :], x_rows[:, r, :])
            last.then_inc(s_dst, 1)
            dve.wait_ge(s_dst, 1)
            for r in range(RT):
                last = dve.bn_aggr(mv[:, r, :], st[:, r, :])
            last.then_inc(s_dst, 1)
            dve.wait_ge(s_dst, 2)
            link(dve.tensor_scalar(ve[:], mv[:, :, 1], LN_EPS, None, ALU.add))
            dve.wait_ge(s_oact, 2)
            newton(lambda n, ins: link(ins), rs1[:], rs0[:], ve[:])
            for r in range(RT):
                last = dve.tensor_scalar(x0[:, r, :], x_rows[:, r, :], mv[:, r, 0:1], rs0[:, r:r + 1],
                                         ALU.subtract, ALU.mult)
            link(last)

            def opening(j):
                if j == 1:
                    for m in range(1, TILES, 2):
                        open_copy(O_WK + m, wkT[:, m, :], lambda bk: bk[:, 0:2 * P])
                    open_copy(O_X + 1, xT0[:, 1, :], lambda bk: bk[:])
                if j in (2, 3, 4, 5):
                    m = 2 * (j - 2) + 1
                    if m >= 2:
                        dve.wait_ge(s_qst[m % 2], 16 * (m // 2))
                    open_copy(O_Q + m, q_stage[m % 2], lambda bk: bk[:], scale=DH ** -0.5)
                if j == 6:
                    open_copy(O_DTW, dtwT[:], lambda bk: bk[0:RANK, 0:DM])
                    dve.wait_ge(s_ws, 16 * 7)
                    link(dve.tensor_tensor(x_rows[:], x_rows[:], bo_r.unsqueeze(1).broadcast_to([P, RT, DM]), ALU.add))
                if j == 7:
                    dve.wait_ge(s_oact, 3)
                    link(dve.tensor_scalar(negA[:], negA[:], -1.0, None, ALU.mult))
                    dve.wait_ge(s_oev[OPEN_DVE], sum(w == OPEN_DVE for w in OPEN_BY))
                    dve.sem_inc(s_opened, 1)

            weight = fw_rows.rearrange("p h d -> p (h d)")
            w_tmp = [flat(hs[i])[:, 2 * DM * n:2 * DM * n + 2 * DM] for i in range(2) for n in range(2)]
            weight_ops = mx_quantize(weight, w_tmp[0], *w_tmp[1:], ypart[0][:, 0, 0, 0:2 * DM // FP6_BLOCK], ypart[0][:, 0, 1, 0:2 * DM // FP6_BLOCK])
            weight_ops.append(lambda: dve.tensor_copy(weight, w_tmp[0]))

            def low_of_group(t, g):
                k0, n = GROUPS[g]
                dve.wait_ge(s_ptH, NG * t + g + 1)
                dve.tensor_tensor(ptL[g % 2][:, 0:n, :], pt_bank[g % 2][:, 0:n * P].rearrange("p (n q) -> p n q", n=n),
                                  ptH[g % 2][:, 0:n, :].bitcast(F32), ALU.subtract).then_inc(s_ptL, 1)

            def chunk_max(t, c):
                _, n = CHUNKS[c]
                dve.wait_ge(s_scores, NG * t + c + 1)
                dve.tensor_reduce(cmax[:, c:c + 1], bank[c][:, 0:n], AX.X, ALU.max).then_inc(s_cmax, 1)

            def reduce_slice(batch, par, s):
                dve.wait_ge(s_hc, SLICES * batch + s + 1)
                dve.tensor_reduce(ypart[par][:, s % 2, s // 2, :], hs[s % 2][:].rearrange("p n q -> p q n"),
                                  AX.X, ALU.add).then_inc(s_red, 1)

            def ffn_link(b, n, ins):
                ins.then_inc(s_fch, 1)
                dve.wait_ge(s_fch, FFN_STEPS * (b - 3) + n + 1)

            def ffn_ops(par, b, j):
                h = half(par)
                r = residual(b - 3, par)
                v, mean = fq[0][h, :], mv[h, 1, 0:1]
                quant = mx_quantize(v, v, fq[1][h, :], xln[h, 0, :], xln[h, 1, :], fscale[h, 0, :], fscale[h, 1, :])
                if j == 1:
                    settle(dve)
                    ffn_link(b, 0, dve.bn_stats(st[h, 1, :], r))
                    settle(dve)
                    ffn_link(b, 1, dve.bn_aggr(mv[h, 1, :], st[h, 1, :]))
                    dve.tensor_scalar(ve[h, 2:3], mv[h, 1, 1:2], LN_EPS, None, ALU.add).then_inc(s_fvar, 1)
                if j == 2:
                    r0, r1 = rs0[h, 2:3], rs1[h, 2:3]
                    dve.wait_ge(s_frsq, b - 2)
                    newton(lambda n, ins: ffn_link(b, 2 + n, ins), r1, r0, ve[h, 2:3])
                    ffn_link(b, 6, dve.tensor_scalar(v, r, mean, r0, ALU.subtract, ALU.mult))
                if j == 3:
                    ffn_link(b, 7, dve.tensor_tensor(r, r, bias_r[h, :], ALU.add))
                for i in {3: (0, 1, 2), 4: (3, 4), 5: (5, 6, 7, 8, 9), 6: (10, 11, 12, 13, 14, 15)}.get(j, ()):
                    if i == 5:
                        dve.wait_ge(s_t2, min(b, NB) if isinstance(b, int) else b)
                    ffn_link(b, 8 + i, quant[i]())
                if j == 6:
                    quant[16]().then_inc(s_fq, 1)

            def body(b, par):
                nxt = 1 - par
                B = b - 1
                if isinstance(b, int) and b == 0:
                    dve.wait_ge(s_opened, 5)
                for j in range(TILES):
                    t = TILES * b + j
                    if isinstance(b, int) and b == FIRST:
                        opening(j)
                    if tile_live(b, j, -1):
                        i = (j + 1) % 2
                        dve.wait_ge(s_qpH, t + 2)
                        dve.tensor_tensor(qpL[i][:].rearrange("p a q -> p (a q)"), misc[:, 0:2 * P],
                                          qpH[i][:].rearrange("p a q -> p (a q)").bitcast(F32), ALU.subtract).then_inc(s_misc, 1)
                    if tile_live(b, j, 2):
                        dve.wait_ge(s_pv, NG * (t - 1))
                        dve.reciprocal(rinv[:], o_bank[:, DC:DC + 1]).then_inc(s_och, 1)
                        dve.wait_ge(s_och, 2 * (t - 2) + 1)
                        dve.tensor_scalar(olow[:], o_bank[:, RH:RW], rinv[:], None, ALU.mult).then_inc(s_och, 1)
                        dve.wait_ge(s_och, 2 * (t - 2) + 2)
                        wait(dve, s_oT, t - 3)
                        dve.scalar_tensor_tensor(osb[j % 2][:], o_bank[:, 0:DC], rinv[:], olow[:],
                                                 ALU.mult, ALU.add).then_inc(s_o, 1)
                    if tile_live(b, j, 0):
                        chunk_max(t, 0)
                    if tile_live(b, j, 1):
                        low_of_group(t - 1, 0)
                    if tile_live(b, j, 0):
                        chunk_max(t, 1)
                    if batch_live(b, 3) and j == 0:
                        if not late(b - 3, SLICES - 1):
                            reduce_slice(b - 3, nxt, SLICES - 1)
                        dve.wait_ge(s_red, SLICES * (b - 2))
                        dve.tensor_reduce(yT[:], ypart[nxt][:].rearrange("p h g q -> p h q g"), AX.X, ALU.add).then_inc(s_y, 1)
                    if batch_live(b, 2) and j >= 1 and not late(b - 2, j - 1):
                        reduce_slice(b - 2, par, j - 1)
                    if tile_live(b, j, 1):
                        low_of_group(t - 1, 1)
                    if batch_live(b, -1):
                        g = j // 2
                        k0, n = GROUPS[g]
                        w = min(n * P, NK - k0 * P)
                        dve.wait_ge(s_ctH, 8 * (b + 1) + j + 1)
                        if j % 2 == 0:
                            dve.tensor_tensor(ctL[nxt][:, k0 * P:k0 * P + w], misc[:, 0:w],
                                              ctH[nxt][:, k0 * P:k0 * P + w].bitcast(F32), ALU.subtract).then_inc(s_misc, 1)
                        else:
                            v = ctT[nxt][DT:P, k0 * P:k0 * P + w]
                            dve.tensor_tensor(v, misc[DT:P, 0:w], v.bitcast(F32), ALU.subtract).then_inc(s_misc, 1)
                    if tile_live(b, j, 0):
                        chunk_max(t, 2)
                    if tile_live(b, j, 1):
                        low_of_group(t - 1, 2)
                    if tile_live(b, j, 0):
                        chunk_max(t, 3)
                        dve.wait_ge(s_cmax, NG * (t + 1))
                        wait(dve, s_exp, NG * t)
                        dve.tensor_reduce(nmax[:, 0:1], cmax[:], AX.X, ALU.max, negate=True).then_inc(s_nmax, 1)
                    if tile_live(b, j, 1):
                        low_of_group(t - 1, 3)
                    if batch_live(b, 3) and j == 1:
                        dve.wait_ge(s_t6, b - 2)
                        r = residual(b - 3, nxt)
                        dve.tensor_tensor(r, misc[half(nxt), 0:DM], r, ALU.add).then_inc(s_misc, 1)
                        dve.wait_ge(s_misc, misc_before(b, j, "y") + 1)
                    if batch_live(b, 3):
                        ffn_ops(nxt, b, j)
                    if batch_live(b, 3) and j == 7:
                        dve.wait_ge(s_fmm, b - 2)
                        r = residual(b - 3, nxt)
                        dve.tensor_tensor(r, misc[half(nxt), 0:DM], r, ALU.add).then_inc(s_misc, 1)
                    if isinstance(b, int) and b == 0:
                        for ins in weight_ops[3 * j:3 * j + 3]:
                            link(ins())
                        if j == len(weight_ops) // 3:
                            dve.sem_inc(s_fwq, 1)
                    if batch_live(b, 1) and j == 2:
                        h = half(nxt)
                        r = residual(B, nxt)
                        dve.wait_ge(s_t1, b)
                        dve.tensor_tensor(r, misc[h, 0:DM], r, ALU.add).then_inc(s_misc, 1)
                        dve.wait_ge(s_misc, misc_before(b, j, "tail") + 1)
                        k = TAIL_STEPS * B
                        settle(dve)
                        dve.bn_stats(st[h, 0, :], r).then_inc(s_tch, 1)
                        dve.wait_ge(s_tch, k + 1)
                        settle(dve)
                        dve.bn_aggr(mv[h, 0, :], st[h, 0, :]).then_inc(s_tch, 1)
                        dve.wait_ge(s_tch, k + 2)
                        dve.tensor_scalar(ve[h, 0:1], mv[h, 0, 1:2], LN_EPS, None, ALU.add)
                        dve.tensor_scalar(ve[h, 1:2], mv[h, 0, 1:2], 1.0 + RMS_EPS, RMS_EPS * LN_EPS,
                                          ALU.mult, ALU.add).then_inc(s_var, 1)
                    if batch_live(b, 2):
                        s = j
                        k = SLICES * (b - 2) + s
                        dve.wait_ge(s_dA, k + 1)
                        dve.wait_ge(s_u, k + 1)
                        hflat = hs[s % 2][:].rearrange("p n q -> p (n q)")
                        dve.tensor_tensor_scan(out=hflat, data0=dA[s % 2][:].rearrange("p n q -> p (n q)"), data1=hflat,
                                               initial=0.0, op0=ALU.mult, op1=ALU.add).then_inc(s_scan, 1)
                        if late(b - 2, s):
                            dve.wait_ge(s_scan, k + 1)
                            dve.wait_ge(s_bcr[s // 2 % 2], 16 * (2 * (b - 2) + s // 4 + 1))
                            dve.tensor_tensor(hs[s % 2][:], hs[s % 2][:],
                                              bcr[s // 2 % 2][:, 1, :].rearrange("p (n q) -> p n q", n=NS),
                                              ALU.mult).then_inc(s_hc, 1)
                            reduce_slice(b - 2, par, s)
                    if batch_live(b, 1) and j == 3:
                        h = half(nxt)
                        r = residual(B, nxt)
                        k = TAIL_STEPS * B + 2
                        dve.wait_ge(s_rsq, b)
                        dve.tensor_tensor(rs0[h, 0:2], rs1[h, 0:2], rs1[h, 0:2], ALU.mult).then_inc(s_tch, 1)
                        dve.wait_ge(s_tch, k + 1)
                        dve.tensor_tensor(rs0[h, 0:2], rs0[h, 0:2], ve[h, 0:2], ALU.mult).then_inc(s_tch, 1)
                        dve.wait_ge(s_tch, k + 2)
                        dve.tensor_scalar(rs0[h, 0:2], rs0[h, 0:2], -0.5, 1.5, ALU.mult, ALU.add).then_inc(s_tch, 1)
                        dve.wait_ge(s_tch, k + 3)
                        dve.tensor_tensor(rs0[h, 0:2], rs0[h, 0:2], rs1[h, 0:2], ALU.mult).then_inc(s_tch, 1)
                        dve.wait_ge(s_tch, k + 4)
                        for i in range(2):
                            last = dve.tensor_scalar(xln[h, i, :], r, mv[h, 0, 0:1], rs0[h, i:i + 1], ALU.subtract, ALU.mult)
                        last.then_inc(s_norm, 1)
                    if batch_live(b, 1) and j == 7:
                        dve.wait_ge(s_sp, 2 * b)
                        dve.scalar_tensor_tensor(dt_[nxt][:], zdt[:], 0.0, sp1[:], ALU.max, ALU.add).then_inc(s_tch, 1)
                        dve.wait_ge(s_tch, TAIL_STEPS * b)
                        dve.tensor_tensor(dtx[nxt][:], dt_[nxt][:], xnT[:], ALU.mult).then_inc(s_dt, 1)

            pipeline(dve, body)

        @block.tensor
        def _(pe):
            def open_use(k):
                who, n, bk = open_place(k)
                wait(pe, s_oev[who], n - 1)
                return s_ope[who], bk

            def transpose_square(bk, src):
                for h in range(2):
                    for o in range(2):
                        last = pe.transpose(bk[:, DM * h + P * o:DM * h + P * o + P], src[:, o, P * h:P * h + P], ident[:])
                return last

            def opening(j):
                if j == 0:
                    pe.wait_ge(s_ident, 1)
                if j == 1:
                    pe.wait_ge(s_wk, 32)
                    for m in range(TILES):
                        done, bk = open_use(O_WK + m)
                        pe.transpose(bk[:, 0:P], wk_a[:, m * P:m * P + P], ident[:])
                        pe.transpose(bk[:, P:DC], wk_b[:, m * P:m * P + P], ident[0:DT, 0:DT])
                        pe.transpose(bk[:, DC:2 * P], wk_b[:, m * P:m * P + P], ident[0:DT, 0:DT]).then_inc(done, 1)
                    pe.wait_ge(s_odve, O_LN0)
                    for h in range(2):
                        done, bk = open_use(O_X + h)
                        for r in range(RT):
                            last = pe.transpose(bk[:, P * r:P * r + P], x0[:, r, P * h:P * h + P], ident[:])
                        last.then_inc(done, 1)
                if j in (2, 3, 4, 5):
                    if j == 2:
                        for h in range(2):
                            who, n, _ = open_place(O_X + h)
                            pe.wait_ge(s_oev[who], n + 1)
                        pe.wait_ge(s_wq, 32)
                    for m in (2 * (j - 2), 2 * (j - 2) + 1):
                        done, bk = open_use(O_Q + m)
                        pe.matmul(bk[:], wq_v[0][:, m * P:m * P + P], xT0[:, 0, :], start=True, stop=False)
                        pe.matmul(bk[:], wq_v[1][:, m * P:m * P + P], xT0[:, 1, :], start=False, stop=True).then_inc(done, 1)
                if j == 6:
                    pe.wait_ge(s_ws, 16 * 7)
                    done, bk = open_use(O_XP)
                    XP = RANK + 2 * STATE
                    for h in range(2):
                        pe.transpose(bk[:, XP * h:XP * h + RANK], xp_dt[:, P * h:P * h + P], ident[0:RANK, 0:RANK])
                        last = pe.transpose(bk[:, XP * h + RANK:XP * h + XP], xp_bc[:, P * h:P * h + P], ident[:])
                    last.then_inc(done, 1)
                    done, bk = open_use(O_DTW)
                    for h in range(2):
                        last = pe.transpose(bk[0:RANK, P * h:P * h + P], dtw_rows[:, h, :], ident[:])
                    last.then_inc(done, 1)
                    done, bk = open_use(O_OP)
                    transpose_square(bk, op_rows).then_inc(done, 1)
                if j == 7:
                    for who in range(2):
                        pe.wait_ge(s_oev[who], sum(w == who for w in OPEN_BY))
                    pe.sem_inc(s_opened, 1)

            def transpose_group(t, g):
                k0, n = GROUPS[g]
                pe.wait_ge(s_exp, NG * t + g + 1)
                wait(pe, s_ptL, NG * t + g - 1)
                for k in range(n):
                    m = key_rows(k0 + k)
                    last = pe.transpose(pt_bank[g % 2][0:m, k * P:k * P + P], prob[:, (k0 + k) * P:(k0 + k) * P + m], ident[:])
                last.then_inc(s_pt, 1)

            def pv_group(t, g, ctx_rows):
                k0, n = GROUPS[g]
                pe.wait_ge(s_ptL, NG * t + g + 1)
                if g == 0:
                    wait(pe, s_o, t)
                for k in range(n):
                    m = key_rows(k0 + k)
                    pe.matmul(o_bank[:, 0:RW], ptH[g % 2][0:m, k, :], ctx_rows[0:m, k0 + k, :],
                              start=k0 + k == 0, stop=False)
                    last = pe.matmul(o_bank[:, 0:RH], ptL[g % 2][0:m, k, :], ctx_rows[0:m, k0 + k, 0:RH],
                                     start=False, stop=k0 + k == KT - 1)
                last.then_inc(s_pv, 1)

            def scores(t, i, par, c):
                c0, n = CHUNKS[c]
                n += n % 2
                wait(pe, s_exp, NG * (t - 1) + c + 1)
                if c == NG - 1:
                    wait(pe, s_aoc, t - 2)
                o = bank[c][:, 0:n]
                keys = slice(c0, c0 + n)
                pe.matmul(o, qpH[i][:, 0, :], ctH[par][:, keys], start=True, stop=False)
                pe.matmul(o, qpH[i][:, 0, :], ctL[par][:, keys], start=False, stop=False)
                pe.matmul(o, qpL[i][:, 0, :], ctH[par][:, keys], start=False, stop=False)
                pe.matmul(o, qpH[i][:, 1, :], ctT[par][:, keys], start=False, stop=False)
                pe.matmul(o, qpL[i][:, 1, :], ctT[par][:, keys], start=False, stop=True).then_inc(s_scores, 1)

            def body(b, par):
                nxt = 1 - par
                B = b - 1
                if isinstance(b, int) and b == 0:
                    pe.wait_ge(s_opened, 5)
                    pe.wait_ge(s_w, 16 * 7)
                for j in range(TILES):
                    t = TILES * b + j
                    tl = (j - 3) % TILES
                    if isinstance(b, int) and b == FIRST:
                        opening(j)
                    if tile_live(b, j, -1) or tile_live(b, j, 0):
                        wait(pe, s_misc, misc_before(b, j, "q"))
                    if tile_live(b, j, -1):
                        i = (j + 1) % TILES
                        qb = qd[par if j < TILES - 1 else nxt]
                        if j == TILES - 1:
                            if par == 0:
                                pe.wait_ge(s_qd[1], 16 * (b + 2))
                            else:
                                pe.wait_ge(s_qd[0], 16 * (b + 3))
                        pe.matmul(misc[:, 0:P], wkT[:, i, 0:P], qb[:, i, :], start=True, stop=True)
                        pe.matmul(misc[:, P:2 * P], wkT[:, i, P:2 * P], qb[:, i, :], start=True, stop=True).then_inc(s_qp, 1)
                    if tile_live(b, j, 2):
                        pv_group(t - 2, 3, rows[par if j >= 2 else nxt])
                    if tile_live(b, j, 0):
                        scores(t, j % 2, par, 0)
                    if tile_live(b, j, 1):
                        transpose_group(t - 1, 0)
                    if tile_live(b, j, 3):
                        wait(pe, s_misc, misc_before(b, j, "oT"))
                        pe.wait_ge(s_o, t - 2)
                        pe.transpose(misc[:, 0:P], osb[(j + 1) % 2][:, 0:P], ident[:])
                        pe.transpose(misc[0:DT, P:2 * P], osb[(j + 1) % 2][:, P:DC], ident[:]).then_inc(s_oT, 1)
                    if tile_live(b, j, 0):
                        scores(t, j % 2, par, 1)
                    if tile_live(b, j, 1):
                        transpose_group(t - 1, 1)
                    if batch_live(b, -1):
                        g = j // 2
                        k0, n = GROUPS[g]
                        wait(pe, s_misc, misc_before(b, j, "ctx"))
                        pe.wait_ge(s_raw[g % 2], raw_loaded(b + 1, g))
                        for k in range(n):
                            m = key_rows(k0 + k)
                            if j % 2 == 0:
                                src = raw[g % 2][0:m, k, 0:P]
                            else:
                                src = raw[g % 2][0:m, k, P:]
                            last = pe.transpose(misc[:, k * P:k * P + m], src, ident[0:m, 0:m])
                        last.then_inc(s_ct, 1)
                    pv_rows = rows[par if j else nxt]
                    if tile_live(b, j, 1) and j == 1:
                        pe.wait_ge(s_rowL, NG * (b + 1))
                    if tile_live(b, j, 1):
                        pv_group(t - 1, 0, pv_rows)
                    if tile_live(b, j, 0):
                        scores(t, j % 2, par, 2)
                    if tile_live(b, j, 1):
                        transpose_group(t - 1, 2)
                    if tile_live(b, j, 3):
                        pe.wait_ge(s_exp, NG * (min(t, NT) if isinstance(t, int) else t))
                        pe.wait_ge(s_misc, misc_before(b, j, "oT") + 1)
                        for h in range(2):
                            q = slice(NQ * h, NQ * h + NQ)
                            c = tl * P + DH * h
                            pe.matmul(ao_bank[q, 0:NQ], wv_a[:, c:c + DH], oT[:, 0, q], start=True, stop=False)
                            last = pe.matmul(ao_bank[q, 0:NQ], wv_b[:, c:c + DH], oT[0:DT, 1, q], start=False, stop=True)
                        last.then_inc(s_ao, 1)
                    if tile_live(b, j, 1):
                        pv_group(t - 1, 1, pv_rows)
                    if tile_live(b, j, 0):
                        scores(t, j % 2, par, 3)
                    if tile_live(b, j, 1):
                        transpose_group(t - 1, 3)
                    if batch_live(b, 1) and j == 2:
                        pe.wait_ge(s_misc, misc_before(b, j, "tail"))
                        pe.wait_ge(s_aoc, TILES * b)
                        for m in range(TILES):
                            last = pe.matmul(misc[half(nxt), 0:DM], ao[nxt][:, m, :], wo[:, m, :],
                                             start=m == 0, stop=m == TILES - 1)
                        last.then_inc(s_t1, 1)
                    if batch_live(b, 1) and j == 4:
                        pe.wait_ge(s_misc, misc_before(b, j, "tail"))
                        pe.wait_ge(s_norm, b)
                        settle(pe)
                        h0 = half(nxt)
                        for i in range(4):
                            last = pe.transpose(misc[:, NQ * i:NQ * i + NQ], xln[h0, i // 2, P * (i % 2):P * (i % 2) + P],
                                                ident[h0, h0])
                        last.then_inc(s_t2, 1)
                    if batch_live(b, 1) and j == 5:
                        pe.wait_ge(s_misc, misc_before(b, j, "tail"))
                        for h in range(2):
                            pe.matmul(misc[:, 0:NQ], xpT[:, h, RANK:], xnT[:, h, :], start=h == 0, stop=h == 1)
                        for h in range(2):
                            last = pe.matmul(misc[0:RANK, NQ:2 * NQ], xpT[:, h, 0:RANK], xnT[:, h, :], start=h == 0, stop=h == 1)
                        last.then_inc(s_t4, 1)
                    if batch_live(b, 1) and j == 6:
                        pe.wait_ge(s_misc, misc_before(b, j, "tail"))
                        for h in range(2):
                            last = pe.matmul(misc[:, NQ * h:NQ * h + NQ], dtwT[:, P * h:P * h + P], dlo[:], start=True, stop=True)
                        last.then_inc(s_t5, 1)
                    if batch_live(b, 3) and j == 1:
                        pe.wait_ge(s_misc, misc_before(b, j, "y"))
                        pe.wait_ge(s_y, b - 2)
                        for h in range(2):
                            last = pe.matmul(misc[half(nxt), 0:DM], yT[:, h, :], opT[:, h, :], start=h == 0, stop=h == 1)
                        last.then_inc(s_t6, 1)
                    if isinstance(b, int) and b == 0 and j == 7:
                        pe.wait_ge(s_misc, misc_before(b, j, "fw"))
                        pe.wait_ge(s_fwq, 1)
                        transpose_square(misc, fw_rows).then_inc(s_fwT, 1)
                    if batch_live(b, 3) and j == 7:
                        pe.wait_ge(s_misc, misc_before(b, j, "fT"))
                        pe.wait_ge(s_fq, b - 2)
                        settle(pe)
                        h0 = half(nxt)
                        for i in range(2):
                            last = pe.transpose(misc[:, NQ * i:NQ * i + NQ], fq[0][h0, P * i:P * i + P], ident[h0, h0])
                        last.then_inc(s_fT, 1)
                    if tile_live(b, j, 1):
                        pv_group(t - 1, 2, pv_rows)
                    if batch_live(b, 3) and j == 7:
                        pe.wait_ge(s_misc, misc_before(b, j, "fmm"))
                        for h in range(2):
                            last = pe.matmul(misc[half(nxt), 0:DM], fqT[:, h, :], wdT[:, h, :], start=h == 0, stop=h == 1)
                        last.then_inc(s_fmm, 1)

            pipeline(pe, body)


_INS = ['x', 'ctx_768', 'L0_xattn_Wq', 'L0_xattn_Wk', 'L0_xattn_Wv', 'L0_xattn_Wo', 'L0_xattn_bo',
        'L0_attn_norm_w', 'L0_attn_x_proj_w', 'L0_attn_dt_proj_w', 'L0_attn_dt_proj_b', 'L0_attn_A_log',
        'L0_attn_D', 'L0_attn_out_proj_w', 'L0_ffn_weight', 'L0_ffn_bias']


def kernel(**inputs):
    import numpy as _np
    import concourse.bacc as _bacc
    from concourse import mybir as _mybir
    from concourse.bass_utils import run_bass_kernel_spmd as _run

    nc = _bacc.Bacc("TRN2", target_bir_lowering=False, num_devices=1)
    arrays, args = {}, []
    for name in _INS:
        a = _np.ascontiguousarray(inputs[name])
        arrays[f"in_{name}"] = a
        args.append(nc.dram_tensor(f"in_{name}", a.shape, _mybir.dt.from_np(a.dtype), kind="ExternalInput").ap())
    shape = inputs['x'].shape
    o = nc.dram_tensor("out_0", shape, _mybir.dt.float32, kind="ExternalOutput").ap()
    perceiver_layer(nc, *args, o)
    r = _run(nc, [arrays], core_ids=[0])
    return r.results[0]["out_0"]
```
